# Optimizing a Trainium2 kernel written in Bass

```python
import numpy as np
import jax
import jax.numpy as jnp

def _softmax(x, axis=-1):
    return jax.nn.softmax(x, axis=axis)

def _gelu(x):
    return jax.nn.gelu(x, approximate=True)

def _silu(x):
    return jax.nn.silu(x)

def _sigmoid(x):
    return jax.nn.sigmoid(x)

def _layernorm(x, axis=-1, eps=1e-05):
    m = jnp.mean(x, axis=axis, keepdims=True)
    v = jnp.var(x, axis=axis, keepdims=True)
    return (x - m) / jnp.sqrt(v + eps)

def _scatter_add(tgt, idx, src, axis=0):
    return tgt.at[idx].add(src)

def _segment_sum(src, seg, n):
    return jax.ops.segment_sum(src, seg, n)
kernel_name = 'mk_decoder_postln_d2_seqx_r4_7d8794'

def setup_inputs(seed: int=0):
    np.random.seed(seed)
    _w = jnp.asarray

    def _rec_inputs():
        import jax
        import jax.numpy as jnp
        _rk = jax.random.key(seed)
        x = 0.0003765 + 1 * jax.random.normal(jax.random.fold_in(_rk, 1), (32, 100, 256), jnp.float32)
        _lenS = 100 - jax.random.randint(jax.random.fold_in(_rk, 7), (32,), 0, max(1, 100 // 4) + 1, jnp.int32)
        _lenS2 = 361 - jax.random.randint(jax.random.fold_in(_rk, 8), (32,), 0, max(1, 361 // 4) + 1, jnp.int32)
        _ctx_1024P = jax.random.normal(jax.random.fold_in(_rk, 11), (32, 16, 256), jnp.float32)
        _ctx_1024c = jax.random.dirichlet(jax.random.fold_in(_rk, 511), 0.3 * jnp.ones((16,), jnp.float32), (32, 361))
        _ctx_1024t = jnp.einsum('bsk,bkd->bsd', _ctx_1024c, _ctx_1024P)
        _ctx_1024t = _ctx_1024t * jax.lax.rsqrt(jnp.mean(jnp.square(_ctx_1024t)) + 1e-12) * 0.953939
        ctx_1024 = -0.000292821 + 1.00034 * (_ctx_1024t + 0.3 * jax.random.normal(jax.random.fold_in(_rk, 611), (32, 361, 256), jnp.float32))
        _validS = jnp.arange(100)[None, :] < _lenS[:, None]
        _validS2 = jnp.arange(361)[None, :] < _lenS2[:, None]
        _causal = jnp.tril(jnp.ones((100, 100), dtype=bool))
        mask_Bx1xSxS2_ik1 = jnp.where(jnp.broadcast_to(_validS2[:, None, None, :], (32, 1, 100, 361)), 1, 0).astype(jnp.int32)
        return (x, ctx_1024, mask_Bx1xSxS2_ik1)
    x, ctx_1024, mask_Bx1xSxS2_ik1 = _rec_inputs()

    def _L0_attn_setup():
        import jax, jax.numpy as jnp
        import numpy as np
        B, S, D_MODEL = (2, 512, 256)
        NUM_HEADS, ATTN_DIM = (16, 64)
        key = jax.random.key(seed)
        ks = jax.random.split(key, 9)
        scale = 1.0 / np.sqrt(D_MODEL)
        states = jax.random.normal(ks[0], (B, S, D_MODEL), dtype=jnp.float32)
        Wq = jax.random.normal(ks[1], (D_MODEL, NUM_HEADS * ATTN_DIM), dtype=jnp.float32) * scale
        bq = jnp.zeros((NUM_HEADS * ATTN_DIM,), dtype=jnp.float32)
        Wk = jax.random.normal(ks[2], (D_MODEL, NUM_HEADS * ATTN_DIM), dtype=jnp.float32) * scale
        bk = jnp.zeros((NUM_HEADS * ATTN_DIM,), dtype=jnp.float32)
        Wv = jax.random.normal(ks[3], (D_MODEL, NUM_HEADS * ATTN_DIM), dtype=jnp.float32) * scale
        bv = jnp.zeros((NUM_HEADS * ATTN_DIM,), dtype=jnp.float32)
        Wo = jax.random.normal(ks[4], (NUM_HEADS * ATTN_DIM, D_MODEL), dtype=jnp.float32) * scale
        bo = jnp.zeros((D_MODEL,), dtype=jnp.float32)
        return {'states': states, 'Wq': Wq, 'bq': bq, 'Wk': Wk, 'bk': bk, 'Wv': Wv, 'bv': bv, 'Wo': Wo, 'bo': bo}
    _L0_attn_all = _L0_attn_setup()
    _L0_attn_in = {k: v for k, v in _L0_attn_all.items() if k in ('Wq', 'bq', 'Wk', 'bk', 'Wv', 'bv', 'Wo', 'bo')}
    del _L0_attn_all

    def _L0_xattn_setup():
        import jax, jax.numpy as jnp
        import numpy as np
        D_MODEL = 256
        HEADS = 16
        D_K = D_MODEL // HEADS
        NEG_INF = -10000000000.0
        key = jax.random.key(seed)
        ks = jax.random.split(key, 10)
        n, s = (2, 512)
        inp = {'value': jax.random.normal(ks[0], (n, s, D_MODEL), dtype=jnp.float32), 'key': jax.random.normal(ks[1], (n, s, D_MODEL), dtype=jnp.float32), 'query': jax.random.normal(ks[2], (n, s, D_MODEL), dtype=jnp.float32), 'mask': jax.random.randint(ks[3], (n, 1, s, s), 0, 2, dtype=jnp.int32), 'Wq': jax.random.normal(ks[4], (D_MODEL, D_MODEL), dtype=jnp.float32) * D_MODEL ** (-0.5), 'Wk': jax.random.normal(ks[5], (D_MODEL, D_MODEL), dtype=jnp.float32) * D_MODEL ** (-0.5), 'Wv': jax.random.normal(ks[6], (D_MODEL, D_MODEL), dtype=jnp.float32) * D_MODEL ** (-0.5), 'Wo': jax.random.normal(ks[7], (D_MODEL, D_MODEL), dtype=jnp.float32) * D_MODEL ** (-0.5), 'bo': jax.random.normal(ks[8], (D_MODEL,), dtype=jnp.float32) * 0.01}
        return inp
    _L0_xattn_all = _L0_xattn_setup()
    _L0_xattn_in = {k: v for k, v in _L0_xattn_all.items() if k in ('Wq', 'Wk', 'Wv', 'Wo', 'bo')}
    del _L0_xattn_all

    def _L0_ffn_setup():
        import jax, jax.numpy as jnp
        import numpy as np
        BLOCK_SIZE = 32
        FP6_E2M3_MAX = 7.5

        def _build_fp6_e2m3_grid():
            vals = set()
            for bits in range(64):
                s = bits >> 5 & 1
                e = bits >> 3 & 3
                m = bits & 7
                v = m / 8.0 if e == 0 else (1.0 + m / 8.0) * 2.0 ** (e - 1)
                vals.add(-v if s else v)
            return np.array(sorted(vals), dtype=np.float32)
        _GRID = jnp.asarray(_build_fp6_e2m3_grid())

        def _nearest_on_grid(x, grid):
            idx = jnp.clip(jnp.searchsorted(grid, x), 0, grid.shape[0] - 1)
            idx_lo = jnp.maximum(idx - 1, 0)
            v_hi = grid[idx]
            v_lo = grid[idx_lo]
            return jnp.where(jnp.abs(x - v_lo) <= jnp.abs(x - v_hi), v_lo, v_hi)

        def _mx_quantize(t, eps=1e-30):
            rows, K = t.shape
            blocks = t.reshape(rows, K // BLOCK_SIZE, BLOCK_SIZE)
            scales = jnp.maximum(jnp.max(jnp.abs(blocks), axis=-1) / FP6_E2M3_MAX, eps)
            q = _nearest_on_grid(blocks / scales[..., None], _GRID)
            return (q, scales)
        key = jax.random.key(seed)
        k1, k2, k3 = jax.random.split(key, 3)
        x = jax.random.normal(k1, (8, 2048, 256), dtype=jnp.float32)
        weight = jax.random.normal(k2, (256, 256), dtype=jnp.float32) * 0.02
        bias = jax.random.normal(k3, (256,), dtype=jnp.float32) * 0.02
        return {'x': x, 'weight': weight, 'bias': bias}
    _L0_ffn_all = _L0_ffn_setup()
    _L0_ffn_in = {k: v for k, v in _L0_ffn_all.items() if k in ('weight', 'bias')}
    del _L0_ffn_all

    def _L1_attn_setup():
        import jax, jax.numpy as jnp
        import numpy as np
        HEADS = 16
        LN_EPS = 1e-05

        def _ln(v, w, b):
            mu = jnp.mean(v, axis=-1, keepdims=True)
            var = jnp.mean(jnp.square(v - mu), axis=-1, keepdims=True)
            return (v - mu) * jax.lax.rsqrt(var + LN_EPS) * w + b
        key = jax.random.key(seed)
        ks = jax.random.split(key, 5)
        b, t, e = (2, 512, 256)
        x = jax.random.normal(ks[0], (b, t, e), dtype=jnp.float32)
        scale = 0.02
        Wk = jax.random.normal(ks[1], (e, e), dtype=jnp.float32) * scale
        Wq = jax.random.normal(ks[2], (e, e), dtype=jnp.float32) * scale
        Wv = jax.random.normal(ks[3], (e, e), dtype=jnp.float32) * scale
        Wu = jax.random.normal(ks[4], (e, e), dtype=jnp.float32) * scale
        s = e // HEADS
        return {'x': x, 'Wk': Wk, 'Wq': Wq, 'Wv': Wv, 'Wu': Wu, 'kln_w': jnp.ones((s,), jnp.float32), 'kln_b': jnp.zeros((s,), jnp.float32), 'qln_w': jnp.ones((s,), jnp.float32), 'qln_b': jnp.zeros((s,), jnp.float32)}
    _L1_attn_all = _L1_attn_setup()
    _L1_attn_in = {k: v for k, v in _L1_attn_all.items() if k in ('Wk', 'Wq', 'Wv', 'Wu', 'kln_w', 'kln_b', 'qln_w', 'qln_b')}
    del _L1_attn_all

    def _L1_xattn_setup():
        import jax, jax.numpy as jnp
        import numpy as np
        D_MODEL = 256
        N_HEADS = 16
        HEAD_DIM = D_MODEL // N_HEADS

        def sparsemax(x):
            x = x - jnp.max(x, axis=-1, keepdims=True)
            zs = -jnp.sort(-x, axis=-1)
            L = x.shape[-1]
            rho = jnp.arange(1, L + 1, dtype=x.dtype)
            cssv = jnp.cumsum(zs, axis=-1) - 1.0
            support = zs > cssv / rho
            k = jnp.maximum(jnp.sum(support, axis=-1, keepdims=True), 1)
            tau = jnp.take_along_axis(cssv, k - 1, axis=-1) / k.astype(x.dtype)
            return jnp.clip(x - tau, 0.0)

        def _split_heads(x):
            B, L, _ = x.shape
            return x.reshape(B, L, N_HEADS, HEAD_DIM).transpose(0, 2, 1, 3)
        key = jax.random.key(seed)
        ks = jax.random.split(key, 11)
        B, L = (2, 512)
        s = 0.02
        inp = {'q': jax.random.normal(ks[0], (B, L, D_MODEL), jnp.float32), 'k': jax.random.normal(ks[1], (B, L, D_MODEL), jnp.float32), 'v': jax.random.normal(ks[2], (B, L, D_MODEL), jnp.float32), 'Wq': jax.random.normal(ks[3], (D_MODEL, D_MODEL), jnp.float32) * s, 'bq': jnp.zeros((D_MODEL,), jnp.float32), 'Wk': jax.random.normal(ks[4], (D_MODEL, D_MODEL), jnp.float32) * s, 'bk': jnp.zeros((D_MODEL,), jnp.float32), 'Wv': jax.random.normal(ks[5], (D_MODEL, D_MODEL), jnp.float32) * s, 'bv': jnp.zeros((D_MODEL,), jnp.float32), 'Wo': jax.random.normal(ks[6], (D_MODEL, D_MODEL), jnp.float32) * s, 'bo': jnp.zeros((D_MODEL,), jnp.float32)}
        return inp
    _L1_xattn_all = _L1_xattn_setup()
    _L1_xattn_in = {k: v for k, v in _L1_xattn_all.items() if k in ('Wq', 'bq', 'Wk', 'bk', 'Wv', 'bv', 'Wo', 'bo')}
    del _L1_xattn_all

    def _L1_ffn_setup():
        import jax, jax.numpy as jnp
        import numpy as np
        H = 256
        I = 512
        E = 32
        B, S = (4, 512)

        def _grouped_mm(a, w, group_sizes):
            return jax.lax.ragged_dot(a, w, group_sizes)

        def _swiglu(x, gw, uw, dw):
            return jax.nn.silu(x @ gw) * (x @ uw) @ dw
        key = jax.random.key(seed)
        ks = jax.random.split(key, 8)
        scale = 0.02
        inp = {'hidden_states': jax.random.normal(ks[0], (B, S, H), dtype=jnp.float32), 'gate_w': jax.random.normal(ks[1], (H, E), dtype=jnp.float32) * scale, 'shared_gate_w': jax.random.normal(ks[2], (H, I), dtype=jnp.float32) * scale, 'shared_up_w': jax.random.normal(ks[3], (H, I), dtype=jnp.float32) * scale, 'shared_down_w': jax.random.normal(ks[4], (I, H), dtype=jnp.float32) * scale, 'routed_gate_w': jax.random.normal(ks[5], (E, H, I), dtype=jnp.float32) * scale, 'routed_up_w': jax.random.normal(ks[6], (E, H, I), dtype=jnp.float32) * scale, 'routed_down_w': jax.random.normal(ks[7], (E, I, H), dtype=jnp.float32) * scale}
        return inp
    _L1_ffn_all = _L1_ffn_setup()
    _L1_ffn_in = {k: v for k, v in _L1_ffn_all.items() if k in ('gate_w', 'shared_gate_w', 'shared_up_w', 'shared_down_w', 'routed_gate_w', 'routed_up_w', 'routed_down_w')}
    del _L1_ffn_all
    return {'x': x, 'ctx_1024': ctx_1024, 'mask_Bx1xSxS2_ik1': mask_Bx1xSxS2_ik1, 'L0_attn_Wq': _L0_attn_in['Wq'], 'L0_attn_bq': _L0_attn_in['bq'], 'L0_attn_Wk': _L0_attn_in['Wk'], 'L0_attn_bk': _L0_attn_in['bk'], 'L0_attn_Wv': _L0_attn_in['Wv'], 'L0_attn_bv': _L0_attn_in['bv'], 'L0_attn_Wo': _L0_attn_in['Wo'], 'L0_attn_bo': _L0_attn_in['bo'], 'L0_xattn_Wq': _L0_xattn_in['Wq'], 'L0_xattn_Wk': _L0_xattn_in['Wk'], 'L0_xattn_Wv': _L0_xattn_in['Wv'], 'L0_xattn_Wo': _L0_xattn_in['Wo'], 'L0_xattn_bo': _L0_xattn_in['bo'], 'L0_ffn_weight': _L0_ffn_in['weight'], 'L0_ffn_bias': _L0_ffn_in['bias'], 'L1_attn_Wk': _L1_attn_in['Wk'], 'L1_attn_Wq': _L1_attn_in['Wq'], 'L1_attn_Wv': _L1_attn_in['Wv'], 'L1_attn_Wu': _L1_attn_in['Wu'], 'L1_attn_kln_w': _L1_attn_in['kln_w'], 'L1_attn_kln_b': _L1_attn_in['kln_b'], 'L1_attn_qln_w': _L1_attn_in['qln_w'], 'L1_attn_qln_b': _L1_attn_in['qln_b'], 'L1_xattn_Wq': _L1_xattn_in['Wq'], 'L1_xattn_bq': _L1_xattn_in['bq'], 'L1_xattn_Wk': _L1_xattn_in['Wk'], 'L1_xattn_bk': _L1_xattn_in['bk'], 'L1_xattn_Wv': _L1_xattn_in['Wv'], 'L1_xattn_bv': _L1_xattn_in['bv'], 'L1_xattn_Wo': _L1_xattn_in['Wo'], 'L1_xattn_bo': _L1_xattn_in['bo'], 'L1_ffn_gate_w': _L1_ffn_in['gate_w'], 'L1_ffn_shared_gate_w': _L1_ffn_in['shared_gate_w'], 'L1_ffn_shared_up_w': _L1_ffn_in['shared_up_w'], 'L1_ffn_shared_down_w': _L1_ffn_in['shared_down_w'], 'L1_ffn_routed_gate_w': _L1_ffn_in['routed_gate_w'], 'L1_ffn_routed_up_w': _L1_ffn_in['routed_up_w'], 'L1_ffn_routed_down_w': _L1_ffn_in['routed_down_w']}

def reference(x, ctx_1024, mask_Bx1xSxS2_ik1, L0_attn_Wq, L0_attn_bq, L0_attn_Wk, L0_attn_bk, L0_attn_Wv, L0_attn_bv, L0_attn_Wo, L0_attn_bo, L0_xattn_Wq, L0_xattn_Wk, L0_xattn_Wv, L0_xattn_Wo, L0_xattn_bo, L0_ffn_weight, L0_ffn_bias, L1_attn_Wk, L1_attn_Wq, L1_attn_Wv, L1_attn_Wu, L1_attn_kln_w, L1_attn_kln_b, L1_attn_qln_w, L1_attn_qln_b, L1_xattn_Wq, L1_xattn_bq, L1_xattn_Wk, L1_xattn_bk, L1_xattn_Wv, L1_xattn_bv, L1_xattn_Wo, L1_xattn_bo, L1_ffn_gate_w, L1_ffn_shared_gate_w, L1_ffn_shared_up_w, L1_ffn_shared_down_w, L1_ffn_routed_gate_w, L1_ffn_routed_up_w, L1_ffn_routed_down_w):
    import jax
    import jax.numpy as jnp

    def _L0_attn_ref(states, Wq, bq, Wk, bk, Wv, bv, Wo, bo):
        import jax, jax.numpy as jnp
        import numpy as np
        B, S, D_MODEL = (2, 512, 256)
        NUM_HEADS, ATTN_DIM = (16, 64)
        b, s, _ = states.shape
        h, d = (NUM_HEADS, ATTN_DIM)

        def proj(W, bias):
            y = jnp.tanh(states @ W + bias)
            return y.reshape(b, s, h, d).transpose(0, 2, 1, 3)
        q, k, v = (proj(Wq, bq), proj(Wk, bk), proj(Wv, bv))
        alpha = jnp.einsum('bhqd,bhkd->bhqk', q, k) / jnp.sqrt(jnp.float32(d))
        causal = jnp.tril(jnp.ones((s, s), dtype=bool))
        alpha = jnp.where(causal, alpha, jnp.finfo(jnp.float32).min)
        alpha = jax.nn.softmax(alpha, axis=-1)
        ctx = jnp.einsum('bhqk,bhkd->bhqd', alpha, v)
        ctx = ctx.transpose(0, 2, 1, 3).reshape(b, s, h * d)
        return jnp.tanh(ctx @ Wo + bo)

    def _L0_xattn_ref(value, key, query, mask, Wq, Wk, Wv, Wo, bo):
        import jax, jax.numpy as jnp
        import numpy as np
        D_MODEL = 256
        HEADS = 16
        D_K = D_MODEL // HEADS
        NEG_INF = -10000000000.0
        n, q_len, _ = query.shape
        q = (query @ Wq.T).reshape(n, q_len, HEADS, D_K)
        k = (key @ Wk.T).reshape(n, key.shape[1], HEADS, D_K)
        v = (value @ Wv.T).reshape(n, value.shape[1], HEADS, D_K)
        scores = jnp.einsum('nqhd,nkhd->nhqk', q, k)
        scores = jnp.where(mask == 0, jnp.float32(NEG_INF), scores)
        attn = jax.nn.softmax(scores / jnp.sqrt(jnp.float32(D_K)), axis=-1)
        out = jnp.einsum('nhql,nlhd->nqhd', attn, v).reshape(n, q_len, D_MODEL)
        return out @ Wo.T + bo

    def _L0_ffn_ref(x, weight, bias):
        import jax, jax.numpy as jnp
        import numpy as np
        BLOCK_SIZE = 32
        FP6_E2M3_MAX = 7.5

        def _build_fp6_e2m3_grid():
            vals = set()
            for bits in range(64):
                s = bits >> 5 & 1
                e = bits >> 3 & 3
                m = bits & 7
                v = m / 8.0 if e == 0 else (1.0 + m / 8.0) * 2.0 ** (e - 1)
                vals.add(-v if s else v)
            return np.array(sorted(vals), dtype=np.float32)
        _GRID = jnp.asarray(_build_fp6_e2m3_grid())

        def _nearest_on_grid(x, grid):
            idx = jnp.clip(jnp.searchsorted(grid, x), 0, grid.shape[0] - 1)
            idx_lo = jnp.maximum(idx - 1, 0)
            v_hi = grid[idx]
            v_lo = grid[idx_lo]
            return jnp.where(jnp.abs(x - v_lo) <= jnp.abs(x - v_hi), v_lo, v_hi)

        def _mx_quantize(t, eps=1e-30):
            rows, K = t.shape
            blocks = t.reshape(rows, K // BLOCK_SIZE, BLOCK_SIZE)
            scales = jnp.maximum(jnp.max(jnp.abs(blocks), axis=-1) / FP6_E2M3_MAX, eps)
            q = _nearest_on_grid(blocks / scales[..., None], _GRID)
            return (q, scales)
        batch_shape = x.shape[:-1]
        in_features = x.shape[-1]
        x2 = x.astype(jnp.float32).reshape(-1, in_features)
        w2 = weight.astype(jnp.float32)
        xq, xs = _mx_quantize(x2)
        wq, ws = _mx_quantize(w2)
        xd = (xq * xs[..., None]).reshape(x2.shape)
        wd = (wq * ws[..., None]).reshape(w2.shape)
        out = xd @ wd.T + bias
        return out.reshape(*batch_shape, -1)

    def _L1_attn_ref(x, Wk, Wq, Wv, Wu, kln_w, kln_b, qln_w, qln_b):
        import jax, jax.numpy as jnp
        import numpy as np
        HEADS = 16
        LN_EPS = 1e-05

        def _ln(v, w, b):
            mu = jnp.mean(v, axis=-1, keepdims=True)
            var = jnp.mean(jnp.square(v - mu), axis=-1, keepdims=True)
            return (v - mu) * jax.lax.rsqrt(var + LN_EPS) * w + b
        b, t, e = x.shape
        h = HEADS
        s = e // h
        k = (x @ Wk.T).reshape(b, t, h, s)
        q = (x @ Wq.T).reshape(b, t, h, s)
        v = (x @ Wv.T).reshape(b, t, h, s)
        k = _ln(k, kln_w, kln_b)
        q = _ln(q, qln_w, qln_b)
        scalefactor = 1.0 / np.sqrt(s).astype(np.float32)
        dot = jnp.einsum('bqhs,bkhs->bhqk', q, k) * scalefactor
        causal = jnp.triu(jnp.ones((t, t), dtype=bool), k=1)
        dot = jnp.where(causal, -jnp.inf, dot)
        attn = jax.nn.softmax(dot, axis=-1)
        out = jnp.einsum('bhqk,bkhs->bqhs', attn, v).reshape(b, t, e)
        return out @ Wu.T

    def _L1_xattn_ref(q, k, v, Wq, bq, Wk, bk, Wv, bv, Wo, bo):
        import jax, jax.numpy as jnp
        import numpy as np
        D_MODEL = 256
        N_HEADS = 16
        HEAD_DIM = D_MODEL // N_HEADS

        def sparsemax(x):
            x = x - jnp.max(x, axis=-1, keepdims=True)
            zs = -jnp.sort(-x, axis=-1)
            L = x.shape[-1]
            rho = jnp.arange(1, L + 1, dtype=x.dtype)
            cssv = jnp.cumsum(zs, axis=-1) - 1.0
            support = zs > cssv / rho
            k = jnp.maximum(jnp.sum(support, axis=-1, keepdims=True), 1)
            tau = jnp.take_along_axis(cssv, k - 1, axis=-1) / k.astype(x.dtype)
            return jnp.clip(x - tau, 0.0)

        def _split_heads(x):
            B, L, _ = x.shape
            return x.reshape(B, L, N_HEADS, HEAD_DIM).transpose(0, 2, 1, 3)
        qh = _split_heads(q @ Wq + bq)
        kh = _split_heads(k @ Wk + bk)
        vh = _split_heads(v @ Wv + bv)
        scale = HEAD_DIM ** (-0.5)
        scores = jnp.einsum('bhqd,bhkd->bhqk', qh, kh) * scale
        attn = sparsemax(scores)
        out = jnp.einsum('bhqk,bhkd->bhqd', attn, vh)
        B, L = (q.shape[0], q.shape[1])
        out = out.transpose(0, 2, 1, 3).reshape(B, L, D_MODEL)
        return out @ Wo + bo

    def _L1_ffn_ref(hidden_states, gate_w, shared_gate_w, shared_up_w, shared_down_w, routed_gate_w, routed_up_w, routed_down_w):
        import jax, jax.numpy as jnp
        import numpy as np
        H = 256
        I = 512
        E = 32
        B, S = (4, 512)

        def _grouped_mm(a, w, group_sizes):
            return jax.lax.ragged_dot(a, w, group_sizes)

        def _swiglu(x, gw, uw, dw):
            return jax.nn.silu(x @ gw) * (x @ uw) @ dw
        b, s, h = hidden_states.shape
        x = hidden_states.reshape(-1, h)
        shared_out = _swiglu(x, shared_gate_w, shared_up_w, shared_down_w)
        logits = x @ gate_w
        topk_ids = jnp.argmax(logits, axis=-1)
        topk_val = jnp.max(logits, axis=-1)
        scores = jax.nn.sigmoid(topk_val)[:, None]
        xs = x * scores
        tokens_per_expert = jnp.zeros((E,), jnp.int32).at[topk_ids].add(1)
        order = jnp.argsort(topk_ids)
        sorted_x = xs[order]
        g = _grouped_mm(sorted_x, routed_gate_w, tokens_per_expert)
        u = _grouped_mm(sorted_x, routed_up_w, tokens_per_expert)
        d = _grouped_mm(jax.nn.silu(g) * u, routed_down_w, tokens_per_expert)
        inv = jnp.argsort(order)
        routed_out = d[inv]
        return (shared_out + routed_out).reshape(b, s, h)
    x = _layernorm(x + _L0_attn_ref(x, L0_attn_Wq, L0_attn_bq, L0_attn_Wk, L0_attn_bk, L0_attn_Wv, L0_attn_bv, L0_attn_Wo, L0_attn_bo), axis=-1)
    x = _layernorm(x + _L0_xattn_ref(ctx_1024, ctx_1024, x, mask_Bx1xSxS2_ik1, L0_xattn_Wq, L0_xattn_Wk, L0_xattn_Wv, L0_xattn_Wo, L0_xattn_bo), axis=-1)
    x = _layernorm(x + _L0_ffn_ref(x, L0_ffn_weight, L0_ffn_bias), axis=-1)
    x = _layernorm(x + _L1_attn_ref(x, L1_attn_Wk, L1_attn_Wq, L1_attn_Wv, L1_attn_Wu, L1_attn_kln_w, L1_attn_kln_b, L1_attn_qln_w, L1_attn_qln_b), axis=-1)
    x = _layernorm(x + _L1_xattn_ref(x, ctx_1024, ctx_1024, L1_xattn_Wq, L1_xattn_bq, L1_xattn_Wk, L1_xattn_bk, L1_xattn_Wv, L1_xattn_bv, L1_xattn_Wo, L1_xattn_bo), axis=-1)
    x = _layernorm(x + _L1_ffn_ref(x, L1_ffn_gate_w, L1_ffn_shared_gate_w, L1_ffn_shared_up_w, L1_ffn_shared_down_w, L1_ffn_routed_gate_w, L1_ffn_routed_up_w, L1_ffn_routed_down_w), axis=-1)
    return x

_drawn_inputs = setup_inputs


def setup_inputs(seed=0):
    import zlib

    import numpy as np

    out = dict(_drawn_inputs(seed))
    spreads = {'L0_attn_bq': (0.0, 0.78),
     'L0_attn_bk': (0.0, 0.8),
     'L0_attn_bv': (0.0, 0.1),
     'L0_attn_bo': (0.0, 0.1),
     'L1_attn_kln_w': (1.0, 0.6),
     'L1_attn_kln_b': (0.0, 2.0),
     'L1_attn_qln_w': (1.0, 0.6),
     'L1_attn_qln_b': (0.0, 0.8),
     'L1_xattn_bq': (0.0, 0.325),
     'L1_xattn_bk': (0.0, 2.0),
     'L1_xattn_bv': (0.0, 0.1),
     'L1_xattn_bo': (0.0, 0.1)}
    factors = {'L0_xattn_bo': 5.747,
     'L0_ffn_bias': 2.929,
     'L1_attn_Wk': 3.61,
     'L1_attn_Wq': 3.597,
     'L1_ffn_gate_w': 5.578,
     'L1_ffn_routed_gate_w': 5.514,
     'L1_ffn_routed_up_w': 5.486,
     'L1_ffn_routed_down_w': 5.483,
     'L1_ffn_shared_gate_w': 8.0,
     'L1_ffn_shared_up_w': 8.0,
     'L1_ffn_shared_down_w': 8.0}
    for name, (base, spread) in spreads.items():
        noise = np.random.default_rng([zlib.crc32(name.encode()), seed]).standard_normal(out[name].shape)
        drawn = base * np.exp(spread * noise) if base else spread * noise
        out[name] = jnp.asarray(drawn.astype(out[name].dtype))
    for name, factor in factors.items():
        out[name] = (out[name] * factor).astype(out[name].dtype)
    return out
```

```python
from contextlib import ExitStack

import numpy as np

import concourse.bass as bass
from concourse import mybir

F32 = mybir.dt.float32
BF16 = mybir.dt.bfloat16
I32 = mybir.dt.int32
ALU = mybir.AluOpType
ACT = mybir.ActivationFunctionType
AX = mybir.AxisListType

P = 128
B = 32
S = 100
D = 256
KD = D // P
S2 = 361
KEYS = [(0, 128), (128, 128), (256, 105)]
ROWS = B * S
LN_EPS = 1e-5
FEW_STEPS = 3
ALL_STEPS = 20
E = 32
TILES = ROWS // P
SLOTS = TILES + E - 1


class Event:

    def __init__(self, place, name, per, credit=0, unit=1, one=1):
        self.sem, self.per, self.unit = place.sem(name), per, unit
        self.credit, self.start = credit, credit * unit + one

    def at(self, i, n):
        assert -self.credit <= n <= self.per, (n, self.credit, self.per)
        return self.sem, i * (self.per * self.unit) + (n * self.unit + self.start)


def is_first(m):
    return isinstance(m, int) and m == 0


def open_all(eng, *events):
    for e in events:
        eng.sem_inc(e.sem, e.start)


class Chain:

    def __init__(self, eng, turns, sem, i, per):
        self.eng, self.turns, self.sem, self.i, self.per, self.n = eng, turns, sem, i, per, 0

    def then(self, ins):
        self.count(ins)
        self.wait()

    def count(self, ins):
        ins.then_inc(self.sem, 1)
        self.n += 1

    def wait(self):
        stand(self.eng, self.turns, self.sem, self.i * self.per + self.n)

    def end(self):
        assert self.n == self.per, (self.n, self.per)


def stand(eng, turns, sem, value):
    eng.wait_ge(sem, value)
    eng.sem_inc(turns, 1)


class Place:

    def __init__(self, nc, ctx, name):
        self.nc, self.ctx, self.name, self.sems = nc, ctx, name, []
        ctx.callback(self.leave)

    def leave(self):
        self.nc.clear_and_free_semaphores(self.sems)
        self.nc.all_engine_barrier()

    def sb(self, name, shape, dt=F32):
        return self.ctx.enter_context(self.nc.sbuf_tensor(f"{self.name}_{name}", shape, dt))

    def psum(self, name, shape=(P, 512), dt=F32):
        return self.ctx.enter_context(self.nc.psum_tensor(f"{self.name}_{name}", list(shape), dt))

    def sem(self, name):
        self.sems.append(self.nc.alloc_semaphore(f"{self.name}_{name}"))
        return self.sems[-1]


def last_bcast(ap, n):
    return ap.unsqueeze(2).to_broadcast([ap.shape[0], ap.shape[1], n])


def mid_bcast(ap, n):
    return ap.unsqueeze(1).to_broadcast([ap.shape[0], n, ap.shape[1]])


def identity(pool, ident, ready, n0):
    pool.memset(ident[:, :], 0.0).then_inc(ready, 1)
    pool.wait_ge(ready, n0 + 1)
    pool.affine_select(out=ident[:, :], in_=ident[:, :], compare_op=ALU.not_equal, fill=1.0, base=0,
                       pattern=[[-1, ident.shape[1]]], channel_multiplier=1).then_inc(ready, 1)


def norm_rows(pool, chain, z, mv, rstd, nbias, half, out, done):
    chain.then(pool.tensor_scalar(rstd, mv[:, 1:2], LN_EPS, None, ALU.add))
    chain.then(pool.tensor_tensor(rstd, rstd, half, ALU.pow))
    chain.then(pool.tensor_tensor(nbias, mv[:, 0:1], rstd, ALU.mult))
    chain.then(pool.tensor_scalar(nbias, nbias, -1.0, None, ALU.mult))
    pool.tensor_scalar(out, z, rstd, nbias, ALU.mult, ALU.add).then_inc(done, 1)


NORM_STEPS = 4


def tanh_attention(nc, x, xT, Wq, bq, Wk, bk, Wv, bv, Wo, bo, out):
    H, HD = 16, 64
    U = 4
    G = B // U
    PAIRS = H // 2
    VW = HD + 1
    with ExitStack() as ctx:
        a = Place(nc, ctx, "ta")
        turns = a.sem("turns")
        wq = a.sb("wq", [P, KD, H * HD])
        wk = a.sb("wk", [P, KD, H * HD])
        wv = a.sb("wv", [P, KD, H * HD])
        wo = a.sb("wo", [P, PAIRS, D])
        bqs = a.sb("bqs", [P, PAIRS])
        bks = a.sb("bks", [P, PAIRS])
        bvs = a.sb("bvs", [P, H * HD])
        bos = a.sb("bos", [P, D])
        ident = a.sb("ident", [P, P])
        half = a.sb("half", [P, 1])
        xTs = a.sb("xTs", [P, KD, U * S])
        xs = a.sb("xs", [S, 2, D])
        qd = a.sb("qd", [P, PAIRS, 2, U * S])
        kT = a.sb("kT", [P, PAIRS, U * S])
        vpre = a.sb("vpre", [S, 2, H * HD])
        v = a.sb("v", [S, 2, H, VW])
        pT = a.sb("pT", [S, 2, H, S])
        rec = a.sb("rec", [S, 2, H])
        o = a.sb("o", [S, 2, H * HD])
        oT = a.sb("oT", [P, 2, PAIRS, S])
        ypre = a.sb("ypre", [S, 2, D])
        z = a.sb("z", [S, 2, D])
        stats = a.sb("stats", [S, 2, 6])
        mv = a.sb("mv", [S, 2, 2])
        rstd = a.sb("rstd", [S, 2, 1])
        nbias = a.sb("nbias", [S, 2, 1])
        xn = a.sb("xn", [S, 2, D])
        proj = [a.psum(f"proj{n}") for n in range(2)]
        sc = [a.psum(f"sc{n}") for n in range(2)]
        pv = [a.psum(f"pv{n}") for n in range(2)]
        tr = a.psum("tr")
        yo = a.psum("yo")

        w_in = a.sem("w_in")
        setup = a.sem("setup")
        xT_in = Event(a, "xT_in", 1, unit=16)
        x_in = [Event(a, f"x_in{n}", U // 2, unit=16) for n in range(2)]
        proj_done = Event(a, "proj_done", 2 * PAIRS + 2 * U)
        qk_done = Event(a, "qk_done", 2 * PAIRS)
        vpre_done = Event(a, "vpre_done", 2 * U, 1)
        v_done = Event(a, "v_done", 2 * U, 3)
        sc_done = Event(a, "sc_done", 4 * U)
        exp_done = Event(a, "exp_done", 4 * U, 1)
        p_done = Event(a, "p_done", 4 * U)
        pv_done = Event(a, "pv_done", 4 * U, 4)
        rec_done = Event(a, "rec_done", 4 * U)
        o_done = Event(a, "o_done", 4 * U, 1)
        tr_done = Event(a, "tr_done", 2 * U, 2)
        oT_done = Event(a, "oT_done", 2 * U)
        yo_done = Event(a, "yo_done", U, 1)
        ypre_done = Event(a, "ypre_done", U)
        y_done = Event(a, "y_done", U)
        z_done = Event(a, "z_done", U, 2)
        st_done = Event(a, "st_done", U)
        mv_done = Event(a, "mv_done", U)
        xn_done = Event(a, "xn_done", U, 1)
        stored = [Event(a, f"stored{n}", U // 2, unit=16) for n in range(2)]
        pool_step = a.sem("pool_step")

        x_g = x.rearrange("(g u s) d -> g u s d", u=U, s=S)
        out_g = out.rearrange("(g u s) d -> g u s d", u=U, s=S)
        xT_g = xT.rearrange("(k p) (g n) -> g p k n", p=P, n=U * S)
        LOADS = 8
        block = ctx.enter_context(nc.Block())

        @block.sync
        def _(sp):
            open_all(sp, xT_in, *x_in, *stored)
            sp.dma_start(wq[:, :, :], Wq.rearrange("(k p) n -> p k n", p=P)).then_inc(w_in, 16)
            sp.dma_start(wk[:, :, :], Wk.rearrange("(k p) n -> p k n", p=P)).then_inc(w_in, 16)
            sp.dma_start(bqs[:, :], bq).then_inc(w_in, 16)
            sp.dma_start(bks[:, :], bk).then_inc(w_in, 16)
            sp.dma_start(wv[:, :, :], Wv.rearrange("(k p) n -> p k n", p=P)).then_inc(w_in, 16)
            sp.dma_start(bvs[:, :], bv).then_inc(w_in, 16)
            sp.dma_start(wo[:, :, :], Wo.rearrange("(k p) n -> p k n", p=P)).then_inc(w_in, 16)
            sp.dma_start(bos[:, :], bo).then_inc(w_in, 16)
            with sp.Fori(0, G) as g:
                sp.wait_ge(*proj_done.at(g, 0))
                sp.dma_start(xTs[:, :, :], xT_g[g]).then_inc(xT_in.sem, 16)
                for u in range(U + 2):
                    if u < U:
                        sp.wait_ge(*z_done.at(g, u - 1))
                        sp.dma_start(xs[:, u % 2, :], x_g[g, u]).then_inc(x_in[u % 2].sem, 16)
                    if u >= 2:
                        sp.wait_ge(*xn_done.at(g, u - 1))
                        sp.dma_start(out_g[g, u - 2], xn[:, u % 2, :]).then_inc(stored[u % 2].sem, 16)
            for n in range(2):
                sp.wait_ge(*stored[n].at(G, 0))

        @block.gpsimd
        def _(pool):
            open_all(pool, p_done, xn_done)
            identity(pool, ident, setup, 0)
            pool.memset(half[:, :], -0.5).then_inc(setup, 1)
            pool.memset(qd[:, :, :, :], 0.0).then_inc(setup, 1)
            pool.memset(v[:, :, :, HD:VW], 1.0).then_inc(setup, 1)
            pool.wait_ge(setup, 5)
            with pool.Fori(0, G) as g:
                chain = Chain(pool, turns, pool_step, g, U * NORM_STEPS)

                def causal(u):
                    for r in range(4):
                        stand(pool, turns, *exp_done.at(g, 4 * u + r + 1))
                        heads = pT[:, u % 2, 4 * r:4 * r + 4, :]
                        pool.affine_select(out=heads, in_=heads, compare_op=ALU.is_ge, fill=0.0, base=0,
                                           pattern=[[0, 4], [1, S]], channel_multiplier=-1).then_inc(p_done.sem, 1)

                def norm(u):
                    pool.wait_ge(*stored[u % 2].at(g, u // 2))
                    stand(pool, turns, *mv_done.at(g, u + 1))
                    norm_rows(pool, chain, z[:, u % 2, :], mv[:, u % 2, :], rstd[:, u % 2, :], nbias[:, u % 2, :],
                              half[0:S, :], xn[:, u % 2, :], xn_done.sem)

                causal(0)
                causal(1)
                causal(2)
                norm(0)
                causal(3)
                norm(1)
                norm(2)
                norm(3)
                chain.end()

        @block.tensor
        def _(pe):
            open_all(pe, proj_done, sc_done, pv_done, tr_done, yo_done)
            pe.wait_ge(w_in, 16 * LOADS)
            pe.wait_ge(setup, 5)
            with pe.Fori(0, G) as g:

                def bank_free(n):
                    if n < 2:
                        pe.wait_ge(*vpre_done.at(g, n - 1))
                    elif n < 2 * PAIRS + 2:
                        pe.wait_ge(*qk_done.at(g, n - 1))
                    else:
                        pe.wait_ge(*vpre_done.at(g, n - 2 * PAIRS - 1))

                def project_qk():
                    pe.wait_ge(*xT_in.at(g, 1))
                    for w, n0 in ((wq, 0), (wk, PAIRS)):
                        for c in range(PAIRS):
                            bank_free(n0 + c)
                            for k in range(KD):
                                mm = pe.matmul(proj[c % 2][:, 0:U * S], w[:, k, c * P:(c + 1) * P], xTs[:, k, :],
                                               start=(k == 0), stop=(k == KD - 1))
                            mm.then_inc(proj_done.sem, 1)

                def project_v(u):
                    for hf in range(2):
                        bank_free(2 * PAIRS + 2 * u + hf)
                        for k in range(KD):
                            mm = pe.matmul(proj[hf][0:S, :], xTs[:, k, u * S:(u + 1) * S],
                                           wv[:, k, hf * 512:(hf + 1) * 512], start=(k == 0), stop=(k == KD - 1))
                        mm.then_inc(proj_done.sem, 1)

                def scores(u):
                    pe.wait_ge(*qk_done.at(g, 2 * PAIRS))
                    for r in range(4):
                        pe.wait_ge(*exp_done.at(g, 4 * u + r - 1))
                        for j in range(2):
                            c = 2 * r + j
                            mm = pe.matmul(sc[r % 2][0:S, j * 2 * S:(j + 1) * 2 * S], kT[:, c, u * S:(u + 1) * S],
                                           qd[:, c, :, u * S:(u + 1) * S], start=True, stop=True)
                        mm.then_inc(sc_done.sem, 1)

                def values(u):
                    pe.wait_ge(*v_done.at(g, 2 * u + 2))
                    for r in range(4):
                        pe.wait_ge(*p_done.at(g, 4 * u + r + 1))
                        pe.wait_ge(*o_done.at(g, 4 * u + r - 1))
                        for j in range(4):
                            h = 4 * r + j
                            mm = pe.matmul(pv[r % 2][0:S, j * VW:(j + 1) * VW], pT[:, u % 2, h, :], v[:, u % 2, h, :],
                                           start=True, stop=True)
                        mm.then_inc(pv_done.sem, 1)

                def turn(u):
                    for t in range(2):
                        pe.wait_ge(*o_done.at(g, 4 * u + 2 * t + 2))
                        pe.wait_ge(*oT_done.at(g, 2 * u + t))
                        for j in range(4):
                            c = 4 * t + j
                            mm = pe.transpose(tr[:, j * S:(j + 1) * S], o[:, u % 2, c * P:(c + 1) * P], ident[0:S, 0:S])
                        mm.then_inc(tr_done.sem, 1)

                def project_out(u):
                    pe.wait_ge(*oT_done.at(g, 2 * u + 2))
                    pe.wait_ge(*ypre_done.at(g, u))
                    for c in range(PAIRS):
                        mm = pe.matmul(yo[0:S, 0:D], oT[:, u % 2, c, :], wo[:, c, :], start=(c == 0), stop=(c == PAIRS - 1))
                    mm.then_inc(yo_done.sem, 1)

                project_qk()
                project_v(0)
                scores(0)
                for u in range(U):
                    if u + 1 < U:
                        project_v(u + 1)
                        scores(u + 1)
                    if u >= 1:
                        turn(u - 1)
                    values(u)
                    if u >= 1:
                        project_out(u - 1)
                turn(U - 1)
                project_out(U - 1)

        @block.scalar
        def _(act):
            open_all(act, qk_done, v_done, exp_done, oT_done, y_done)
            act.wait_ge(w_in, 16 * LOADS)
            act.wait_ge(setup, 5)
            with act.Fori(0, G) as g:

                def tanh_qk():
                    for c in range(PAIRS):
                        act.wait_ge(*proj_done.at(g, c + 1))
                        for e in range(2):
                            r = slice(HD * e, HD * e + HD)
                            ins = act.activation(qd[r, c, e, :], proj[c % 2][r, 0:U * S], ACT.Tanh, bias=bqs[r, c:c + 1])
                        ins.then_inc(qk_done.sem, 1)
                    for c in range(PAIRS):
                        act.wait_ge(*proj_done.at(g, PAIRS + c + 1))
                        act.activation(kT[:, c, :], proj[c % 2][:, 0:U * S], ACT.Tanh,
                                       bias=bks[:, c:c + 1]).then_inc(qk_done.sem, 1)

                def tanh_v(u):
                    act.wait_ge(*pv_done.at(g, 4 * u - 4))
                    for hf in range(2):
                        act.wait_ge(*vpre_done.at(g, 2 * u + hf + 1))
                        act.activation(v[:, u % 2, 8 * hf:8 * hf + 8, 0:HD],
                                       vpre[:, u % 2, 512 * hf:512 * hf + 512].rearrange("p (h d) -> p h d", d=HD),
                                       ACT.Tanh).then_inc(v_done.sem, 1)

                def exps(u):
                    for r in range(4):
                        act.wait_ge(*sc_done.at(g, 4 * u + r + 1))
                        act.activation(pT[:, u % 2, 4 * r:4 * r + 4, :].rearrange("p h s -> p (h s)"),
                                       sc[r % 2][0:S, 0:4 * S], ACT.Exp, scale=HD ** -0.5).then_inc(exp_done.sem, 1)

                def copy_turned(u):
                    act.wait_ge(*yo_done.at(g, u - 1))
                    for t in range(2):
                        act.wait_ge(*tr_done.at(g, 2 * u + t + 1))
                        act.activation(oT[:, u % 2, 4 * t:4 * t + 4, :].rearrange("p c s -> p (c s)"),
                                       tr[:, 0:4 * S], ACT.Copy).then_inc(oT_done.sem, 1)

                def tanh_y(u):
                    act.wait_ge(*ypre_done.at(g, u + 1))
                    act.activation(ypre[:, u % 2, :], ypre[:, u % 2, :], ACT.Tanh).then_inc(y_done.sem, 1)

                tanh_qk()
                tanh_v(0)
                exps(0)
                for u in range(U):
                    if u + 1 < U:
                        tanh_v(u + 1)
                        exps(u + 1)
                    if u >= 1:
                        copy_turned(u - 1)
                        tanh_y(u - 1)
                copy_turned(U - 1)
                tanh_y(U - 1)

        @block.vector
        def _(dve):
            open_all(dve, vpre_done, rec_done, o_done, ypre_done, z_done, st_done, mv_done)
            dve.wait_ge(w_in, 16 * LOADS)
            with dve.Fori(0, G) as g:

                def bias_v(u):
                    for hf in range(2):
                        dve.wait_ge(*v_done.at(g, 2 * u + hf - 3))
                        dve.wait_ge(*proj_done.at(g, 2 * PAIRS + 2 * u + hf + 1))
                        dve.tensor_tensor(vpre[:, u % 2, 512 * hf:512 * hf + 512], proj[hf][0:S, :],
                                          bvs[0:S, 512 * hf:512 * hf + 512], ALU.add).then_inc(vpre_done.sem, 1)

                def normalise(u):
                    dve.wait_ge(*tr_done.at(g, 2 * u - 2))
                    for r in range(4):
                        full = pv[r % 2][0:S, 0:4 * VW].rearrange("p (h d) -> p h d", d=VW)
                        dve.wait_ge(*pv_done.at(g, 4 * u + r + 1))
                        dve.reciprocal(rec[:, u % 2, 4 * r:4 * r + 4], full[:, :, HD]).then_inc(rec_done.sem, 1)
                        dve.wait_ge(*rec_done.at(g, 4 * u + r + 1))
                        dve.tensor_tensor(o[:, u % 2, 256 * r:256 * r + 256].rearrange("p (h d) -> p h d", d=HD),
                                          full[:, :, 0:HD], last_bcast(rec[:, u % 2, 4 * r:4 * r + 4], HD),
                                          ALU.mult).then_inc(o_done.sem, 1)

                def output(u):
                    dve.wait_ge(*yo_done.at(g, u + 1))
                    dve.tensor_tensor(ypre[:, u % 2, :], yo[0:S, 0:D], bos[0:S, :], ALU.add).then_inc(ypre_done.sem, 1)
                    dve.wait_ge(*y_done.at(g, u + 1))
                    dve.wait_ge(*x_in[u % 2].at(g, u // 2 + 1))
                    dve.wait_ge(*xn_done.at(g, u - 1))
                    dve.tensor_tensor(z[:, u % 2, :], ypre[:, u % 2, :], xs[:, u % 2, :], ALU.add).then_inc(z_done.sem, 1)
                    dve.wait_ge(*z_done.at(g, u + 1))
                    dve.bn_stats(stats[:, u % 2, :], z[:, u % 2, :]).then_inc(st_done.sem, 1)
                    stand(dve, turns, *st_done.at(g, u + 1))
                    dve.bn_aggr(mv[:, u % 2, :], stats[:, u % 2, :]).then_inc(mv_done.sem, 1)

                bias_v(0)
                for u in range(U):
                    if u + 1 < U:
                        bias_v(u + 1)
                    normalise(u)
                    if u >= 1:
                        output(u - 1)
                output(U - 1)


def cross_attention(nc, x, cT, mask, heads01, WqT, WkT, WvT, WoT, bo, out):
    H, HD = 16, 16
    HC = P // HD
    NK = len(KEYS)
    LAST = B - 1
    with ExitStack() as ctx:
        a = Place(nc, ctx, "ca")
        wq = a.sb("wq", [P, KD, D])
        wk = a.sb("wk", [P, KD, D])
        wv = a.sb("wv", [P, KD, D])
        wo = a.sb("wo", [P, KD, D])
        bos = a.sb("bos", [P, D])
        hm = a.sb("hm", [P, HC])
        ident = a.sb("ident", [P, P])
        half = a.sb("half", [P, 1])
        cTs = a.sb("cTs", [P, 2, KD, S2])
        xq = a.sb("xq", [S, 2, D])
        xr = a.sb("xr", [S, 2, D])
        ms = a.sb("ms", [S, 2, S2], I32)
        mb = a.sb("mb", [S, 2, S2])
        xT = a.sb("xT", [P, KD * S])
        qs = a.sb("qs", [P, KD, S])
        qm = a.sb("qm", [P, 2, H, S])
        kT = a.sb("kT", [P, 2, KD, S2])
        vm = a.sb("vm", [P, 2, NK, H, 2 * HD])
        sm = a.sb("sm", [S, 2, 4, S2])
        nb = a.sb("nb", [S, 2, 4])
        p = a.sb("p", [S, 2, 4, S2])
        den = a.sb("den", [S, 2, 4])
        rec = a.sb("rec", [S, 2, 4])
        pT = a.sb("pT", [P, 2, NK, 4 * S])
        oT = a.sb("oT", [P, 2, KD * S])
        xb = a.sb("xb", [S, 2, D])
        z = a.sb("z", [S, 2, D])
        stats = a.sb("stats", [S, 2, 6])
        mv = a.sb("mv", [S, 2, 2])
        rstd = a.sb("rstd", [S, 2, 1])
        nbias = a.sb("nbias", [S, 2, 1])
        xn = a.sb("xn", [S, 2, D])
        proj = [a.psum(f"proj{n}") for n in range(2)]
        sc = [a.psum(f"sc{n}") for n in range(2)]
        tr = [a.psum(f"tr{n}") for n in range(2)]
        ov = a.psum("ov")
        yo = a.psum("yo")

        turns = a.sem("turns")
        w_in = a.sem("w_in")
        setup = a.sem("setup")
        xq_in = [Event(a, f"xq_in{n}", 1, unit=16) for n in range(2)]
        cT_in = [Event(a, f"cT_in{n}", 1, unit=16) for n in range(2)]
        ms_in = [Event(a, f"ms_in{n}", 1, unit=16) for n in range(2)]
        xr_in = [Event(a, f"xr_in{n}", 1, unit=16) for n in range(2)]
        stored = [Event(a, f"stored{n}", 1, unit=16) for n in range(2)]
        proj_done = Event(a, "proj_done", 8, 16)
        qk_done = Event(a, "qk_done", 5)
        v_done = Event(a, "v_done", 3, 1)
        qm_done = Event(a, "qm_done", 1)
        mb_done = Event(a, "mb_done", 1, 2)
        sc_done = Event(a, "sc_done", H)
        mx_done = Event(a, "mx_done", H, 1)
        exp_done = Event(a, "exp_done", H, 4)
        rec_done = Event(a, "rec_done", 4)
        pn_done = Event(a, "pn_done", 4)
        tr_done = Event(a, "tr_done", 4 * NK, NK)
        ca_done = Event(a, "ca_done", 2 * NK)
        cd_done = Event(a, "cd_done", 2 * NK)
        ov_done = Event(a, "ov_done", 4, 1)
        oT_done = Event(a, "oT_done", 1)
        yo_done = Event(a, "yo_done", 1, 1)
        xb_done = Event(a, "xb_done", 1, 2)
        z_done = Event(a, "z_done", 1, 1)
        st_done = Event(a, "st_done", 1)
        mv_done = Event(a, "mv_done", 1)
        xn_done = Event(a, "xn_done", 1, 2)
        pool_step = a.sem("pool_step")
        LOADS = 6

        x_s = x.rearrange("(b s) d -> b s d", s=S)
        out_s = out.rearrange("(b s) d -> b s d", s=S)
        cT_s = cT.rearrange("b (k p) n -> b p k n", p=P)


        def prev(m, u):
            return (m, 0) if u else (m - 1, 1)

        block = ctx.enter_context(nc.Block())

        @block.sync
        def _(sp):
            open_all(sp, *xq_in, *cT_in, *ms_in, *xr_in, *stored)
            sp.dma_start(wq[:, :, :], WqT.rearrange("(k p) n -> p k n", p=P)).then_inc(w_in, 16)
            sp.dma_start(wk[:, :, :], WkT.rearrange("(k p) n -> p k n", p=P)).then_inc(w_in, 16)
            sp.dma_start(wv[:, :, :], WvT.rearrange("(k p) n -> p k n", p=P)).then_inc(w_in, 16)
            sp.dma_start(wo[:, :, :], WoT.rearrange("(k p) n -> p k n", p=P)).then_inc(w_in, 16)
            sp.dma_start(bos[:, :], bo).then_inc(w_in, 16)
            sp.dma_start(hm[:, :], heads01).then_inc(w_in, 16)

            def load(m, u):
                n = 2 * m + u
                sp.wait_ge(*proj_done.at(n, -15))
                sp.dma_start(xq[:, u, :], x_s[n]).then_inc(xq_in[u].sem, 16)
                sp.wait_ge(*proj_done.at(n, -8))
                sp.dma_start(cTs[:, u, :, :], cT_s[n]).then_inc(cT_in[u].sem, 16)
                sp.wait_ge(*mb_done.at(n, -1))
                sp.dma_start(ms[:, u, :], mask[n]).then_inc(ms_in[u].sem, 16)

            def load_residual(m, u):
                n = 2 * m + u
                sp.wait_ge(*xb_done.at(n, -1))
                sp.dma_start(xr[:, u, :], x_s[n]).then_inc(xr_in[u].sem, 16)

            def store(m, u):
                n = 2 * m + u
                sp.wait_ge(*xn_done.at(n, 1))
                sp.dma_start(out_s[n], xn[:, u, :]).then_inc(stored[u].sem, 16)

            load(0, 0)
            load(0, 1)
            load_residual(0, 0)
            load_residual(0, 1)
            with sp.Fori(1, B // 2) as m:
                for u in range(2):
                    load(m, u)
                    store(m - 1, u)
                    load_residual(m, u)
            store(B // 2 - 1, 0)
            store(B // 2 - 1, 1)
            for u in range(2):
                sp.wait_ge(*stored[u].at(B // 2, 0))

        def passes(eng, body):
            body(0, 0, behind=False)
            body(0, 1)
            with eng.Fori(1, B // 2 - 1) as m:
                body(m, 0)
                body(m, 1)
            body(B // 2 - 1, 0)
            body(B // 2 - 1, 1, ahead=False)
            body(B // 2, 0, here=False, ahead=False)

        @block.gpsimd
        def _(pool):
            open_all(pool, qm_done, pn_done, xb_done, xn_done)
            identity(pool, ident, setup, 0)
            pool.memset(half[:, :], -0.5).then_inc(setup, 1)
            pool.memset(vm[:, :, :, :, :], 0.0).then_inc(setup, 1)
            pool.wait_ge(setup, 4)
            pool.wait_ge(w_in, 16 * LOADS)

            def part_heads(m, u):
                n = 2 * m + u
                pool.wait_ge(*qk_done.at(n, 3))
                for k in range(KD):
                    ins = pool.tensor_tensor(qm[:, u, HC * k:HC * k + HC, :], mid_bcast(qs[:, k, :], HC),
                                             last_bcast(hm[:, :], S), ALU.mult)
                ins.then_inc(qm_done.sem, 1)

            def probabilities(m, u, r):
                n = 2 * m + u
                stand(pool, turns, *rec_done.at(n, r + 1))
                for j in range(4):
                    ins = pool.tensor_scalar(p[:, r % 2, j, :], p[:, r % 2, j, :], rec[:, r % 2, j:j + 1], 1.0,
                                             ALU.mult, ALU.mult)
                ins.then_inc(pn_done.sem, 1)

            def add_bias(m, u):
                n = 2 * m + u
                pool.wait_ge(*xr_in[u].at(m, 1))
                pool.wait_ge(*z_done.at(n, -1))
                pool.tensor_tensor(xb[:, u, :], xr[:, u, :], bos[0:S, :], ALU.add).then_inc(xb_done.sem, 1)

            def norm(m, u):
                n = 2 * m + u
                chain = Chain(pool, turns, pool_step, n, NORM_STEPS)
                pool.wait_ge(*stored[u].at(m, 0))
                stand(pool, turns, *mv_done.at(n, 1))
                norm_rows(pool, chain, z[:, u, :], mv[:, u, :], rstd[:, u, :], nbias[:, u, :], half[0:S, :],
                          xn[:, u, :], xn_done.sem)
                chain.end()

            def sequence(m, u, behind=True, here=True, ahead=True):
                if here:
                    probabilities(m, u, 0)
                    probabilities(m, u, 1)
                    if ahead:
                        part_heads(*((m, 1) if u == 0 else (m + 1, 0)))
                    add_bias(m, u)
                    probabilities(m, u, 2)
                    probabilities(m, u, 3)
                if behind:
                    norm(*prev(m, u))

            part_heads(0, 0)
            passes(pool, sequence)

        @block.tensor
        def _(pe):
            open_all(pe, proj_done, sc_done, tr_done, ov_done, yo_done)
            pe.wait_ge(w_in, 16 * LOADS)
            pe.wait_ge(setup, 4)

            def bank_free(n, f):
                if f < 2:
                    pe.wait_ge(*v_done.at(n, f - 1))
                elif f < 7:
                    pe.wait_ge(*qk_done.at(n, f - 1))
                else:
                    pe.wait_ge(*v_done.at(n, 1))

            def turn_x(m, u):
                n = 2 * m + u
                pe.wait_ge(*xq_in[u].at(m, 1))
                bank_free(n, 0)
                for k in range(KD):
                    mm = pe.transpose(proj[0][:, k * S:(k + 1) * S], xq[:, u, k * P:(k + 1) * P], ident[0:S, 0:S])
                mm.then_inc(proj_done.sem, 1)

            def project_q(m, u):
                n = 2 * m + u
                pe.wait_ge(*qk_done.at(n, 1))
                for c in range(KD):
                    bank_free(n, 1 + c)
                    for k in range(KD):
                        mm = pe.matmul(proj[(1 + c) % 2][:, 0:S], wq[:, k, c * P:(c + 1) * P], xT[:, k * S:(k + 1) * S],
                                       start=(k == 0), stop=(k == KD - 1))
                    mm.then_inc(proj_done.sem, 1)

            def project_k(m, u):
                n = 2 * m + u
                pe.wait_ge(*cT_in[u].at(m, 1))
                for c in range(KD):
                    bank_free(n, 3 + c)
                    for k in range(KD):
                        mm = pe.matmul(proj[(3 + c) % 2][:, 0:S2], wk[:, k, c * P:(c + 1) * P], cTs[:, u, k, :],
                                       start=(k == 0), stop=(k == KD - 1))
                    mm.then_inc(proj_done.sem, 1)

            def project_v(m, u):
                n = 2 * m + u
                for t, (k0, kn) in enumerate(KEYS):
                    bank_free(n, 5 + t)
                    for k in range(KD):
                        mm = pe.matmul(proj[(5 + t) % 2][0:kn, 0:D], cTs[:, u, k, k0:k0 + kn], wv[:, k, :],
                                       start=(k == 0), stop=(k == KD - 1))
                    mm.then_inc(proj_done.sem, 1)

            def scores(m, u, r):
                n = 2 * m + u
                if r == 0:
                    pe.wait_ge(*qm_done.at(n, 1))
                    pe.wait_ge(*qk_done.at(n, 5))
                for j in range(4):
                    h = 4 * r + j
                    pe.wait_ge(*mx_done.at(n, h - 1))
                    pe.matmul(sc[h % 2][0:S, 0:S2], qm[:, u, h, :], kT[:, u, h // HC, :],
                              start=True, stop=True).then_inc(sc_done.sem, 1)

            def turn(m, u, r, t):
                n = 2 * m + u
                f = NK * r + t
                if t == 0:
                    pe.wait_ge(*pn_done.at(n, r + 1))
                pe.wait_ge(*(cd_done if f % 2 else ca_done).at(n, f // 2))
                k0, kn = KEYS[t]
                for j in range(4):
                    mm = pe.transpose(tr[f % 2][0:kn, j * S:(j + 1) * S], p[:, r % 2, j, k0:k0 + kn], ident[0:S, 0:S])
                mm.then_inc(tr_done.sem, 1)

            def values(m, u, r, t):
                n = 2 * m + u
                f = NK * r + t
                if r == 0 and t == 0:
                    pe.wait_ge(*v_done.at(n, 3))
                    pe.wait_ge(*oT_done.at(n, 0))
                pe.wait_ge(*(cd_done if f % 2 else ca_done).at(n, f // 2 + 1))
                kn = KEYS[t][1]
                for j in range(4):
                    h = 4 * r + j
                    g = h // 2
                    mm = pe.matmul(ov[32 * (g % 4):32 * (g % 4) + 32, (g // 4) * S:(g // 4 + 1) * S],
                                   vm[0:kn, u, t, h, :], pT[0:kn, r % 2, t, j * S:(j + 1) * S],
                                   start=(t == 0 and j % 2 == 0), stop=(t == NK - 1 and j % 2 == 1))
                if t == NK - 1:
                    mm.then_inc(ov_done.sem, 1)

            def project_out(m, u):
                n = 2 * m + u
                pe.wait_ge(*oT_done.at(n, 1))
                pe.wait_ge(*z_done.at(n, 0))
                for k in range(KD):
                    mm = pe.matmul(yo[0:S, 0:D], oT[:, u, k * S:(k + 1) * S], wo[:, k, :], start=(k == 0), stop=(k == KD - 1))
                mm.then_inc(yo_done.sem, 1)

            def sequence(m, u, behind=True, here=True, ahead=True):
                following = (m, 1) if u == 0 else (m + 1, 0)
                for r in range(4 if here else 2):
                    if here:
                        scores(m, u, r)
                    for t in range(NK):
                        if r >= 1:
                            if here:
                                turn(m, u, r - 1, t)
                        elif behind:
                            turn(*prev(m, u), 3, t)
                        if r >= 2:
                            values(m, u, r - 2, t)
                        elif behind:
                            values(*prev(m, u), r + 2, t)
                    if ahead:
                        (turn_x, project_q, project_k, project_v)[r](*following)
                    if behind and r == (2 if here else 1):
                        project_out(*prev(m, u))

            turn_x(0, 0)
            project_q(0, 0)
            project_k(0, 0)
            project_v(0, 0)
            passes(pe, sequence)

        @block.scalar
        def _(act):
            open_all(act, qk_done, exp_done, ca_done, oT_done)
            act.wait_ge(setup, 4)

            def copy_proj(m, u, f):
                n = 2 * m + u
                bank = proj[f % 2]
                act.wait_ge(*proj_done.at(n, f + 1))
                if f == 0:
                    ins = act.activation(xT[:, :], bank[:, 0:KD * S], ACT.Copy)
                elif f < 3:
                    if f == 1:
                        act.wait_ge(*qm_done.at(n, 0))
                    ins = act.activation(qs[:, f - 1, :], bank[:, 0:S], ACT.Copy)
                else:
                    ins = act.activation(kT[:, u, f - 3, :], bank[:, 0:S2], ACT.Copy)
                ins.then_inc(qk_done.sem, 1)

            def exps(m, u, r, j):
                n = 2 * m + u
                if j == 0:
                    act.wait_ge(*tr_done.at(n, NK * (r - 1)))
                act.wait_ge(*mx_done.at(n, 4 * r + j + 1))
                act.activation(p[:, r % 2, j, :], sm[:, r % 2, j, :], ACT.Exp, bias=nb[:, r % 2, j:j + 1], scale=-1.0,
                               accum_out=den[:, r % 2, j:j + 1]).then_inc(exp_done.sem, 1)

            def copy_turned(m, u, r):
                n = 2 * m + u
                act.wait_ge(*ov_done.at(n, r - 1))
                for t, (k0, kn) in enumerate(KEYS):
                    f = NK * r + t
                    if f % 2 == 0:
                        act.wait_ge(*tr_done.at(n, f + 1))
                        act.activation(pT[0:kn, r % 2, t, :], tr[0][0:kn, 0:4 * S], ACT.Copy).then_inc(ca_done.sem, 1)

            def copy_out(m, u):
                n = 2 * m + u
                act.wait_ge(*ov_done.at(n, 4))
                act.wait_ge(*yo_done.at(n, -1))
                act.activation(oT[:, u, :], ov[:, 0:KD * S], ACT.Copy).then_inc(oT_done.sem, 1)

            def sequence(m, u, behind=True, here=True, ahead=True):
                following = (m, 1) if u == 0 else (m + 1, 0)
                for r in range(4 if here else 2):
                    if here:
                        exps(m, u, r, 0)
                        exps(m, u, r, 1)
                    if r >= 1:
                        if here:
                            copy_turned(m, u, r - 1)
                    elif behind:
                        copy_turned(*prev(m, u), 3)
                    if here:
                        exps(m, u, r, 2)
                        exps(m, u, r, 3)
                    if ahead:
                        for f in ((0,), (1, 2), (3, 4), ())[r]:
                            copy_proj(*following, f)
                    if behind and r == 1:
                        copy_out(*prev(m, u))

            for f in range(5):
                copy_proj(0, 0, f)
            passes(act, sequence)

        @block.vector
        def _(dve):
            open_all(dve, v_done, mb_done, mx_done, cd_done, rec_done, z_done, st_done, mv_done)
            dve.wait_ge(w_in, 16 * LOADS)
            dve.wait_ge(setup, 4)

            def copy_v(m, u):
                n = 2 * m + u
                for t, (k0, kn) in enumerate(KEYS):
                    dve.wait_ge(*proj_done.at(n, 6 + t))
                    bank = proj[(5 + t) % 2][0:kn, 0:D].rearrange("p (g e d) -> p g e d", e=2, d=HD)
                    for e in range(2):
                        ins = dve.tensor_copy(vm[0:kn, u, t, e:H:2, HD * e:HD * e + HD], bank[:, :, e, :])
                    ins.then_inc(v_done.sem, 1)

            def mask_bias(m, u):
                n = 2 * m + u
                dve.wait_ge(*ms_in[u].at(m, 1))
                dve.tensor_scalar(mb[:, u, :], ms[:, u, :], 0.0, -1e10, ALU.is_equal, ALU.mult).then_inc(mb_done.sem, 1)

            def maxima(m, u, r):
                n = 2 * m + u
                if r == 0:
                    dve.wait_ge(*mb_done.at(n, 1))
                dve.wait_ge(*exp_done.at(n, 4 * r - 4))
                for j in range(4):
                    h = 4 * r + j
                    stand(dve, turns, *sc_done.at(n, h + 1))
                    dve.tensor_tensor_reduce(sm[:, r % 2, j, :], sc[h % 2][0:S, 0:S2], mb[:, u, :], -1 / 4, 3e38,
                                             ALU.add, ALU.min, nb[:, r % 2, j:j + 1]).then_inc(mx_done.sem, 1)

            def copy_turned(m, u, r):
                n = 2 * m + u
                dve.wait_ge(*ov_done.at(n, r - 1))
                for t, (k0, kn) in enumerate(KEYS):
                    f = NK * r + t
                    if f % 2:
                        dve.wait_ge(*tr_done.at(n, f + 1))
                        dve.tensor_copy(pT[0:kn, r % 2, t, :], tr[1][0:kn, 0:4 * S]).then_inc(cd_done.sem, 1)

            def reciprocals(m, u, r):
                n = 2 * m + u
                dve.wait_ge(*exp_done.at(n, 4 * r + 4))
                dve.reciprocal(rec[:, r % 2, :], den[:, r % 2, :]).then_inc(rec_done.sem, 1)

            def output(m, u):
                n = 2 * m + u
                dve.wait_ge(*yo_done.at(n, 1))
                dve.wait_ge(*xb_done.at(n, 1))
                dve.wait_ge(*xn_done.at(n, -1))
                dve.tensor_tensor(z[:, u, :], yo[0:S, 0:D], xb[:, u, :], ALU.add).then_inc(z_done.sem, 1)
                dve.wait_ge(*z_done.at(n, 1))
                dve.bn_stats(stats[:, u, :], z[:, u, :]).then_inc(st_done.sem, 1)
                stand(dve, turns, *st_done.at(n, 1))
                dve.bn_aggr(mv[:, u, :], stats[:, u, :]).then_inc(mv_done.sem, 1)

            def sequence(m, u, behind=True, here=True, ahead=True):
                following = (m, 1) if u == 0 else (m + 1, 0)
                for r in range(4 if here else 2):
                    if here:
                        maxima(m, u, r)
                    if r >= 1:
                        if here:
                            copy_turned(m, u, r - 1)
                    elif behind:
                        copy_turned(*prev(m, u), 3)
                    if here:
                        reciprocals(m, u, r)
                    if behind and r == (3 if here else 1):
                        output(*prev(m, u))
                    if ahead and r == 3:
                        copy_v(*following)
                        mask_bias(*following)

            copy_v(0, 0)
            mask_bias(0, 0)
            passes(dve, sequence)


def quantised_linear(nc, x, W, bias, out):
    BLOCK = 32
    NB = D // BLOCK
    ROUND = 1.5 * 2.0 ** 23
    STEPS = 16
    with ExitStack() as ctx:
        a = Place(nc, ctx, "ql")
        ws = a.sb("ws", [P, KD, D])
        wd = a.sb("wd", [P, KD, D])
        wT = a.sb("wT", [P, KD, D])
        bs = a.sb("bs", [P, D])
        ident = a.sb("ident", [P, P])
        half = a.sb("half", [P, 1])
        xs = a.sb("xs", [P, 2, D])
        xd = a.sb("xd", [P, 2, D])
        amax = a.sb("amax", [P, NB])
        scale = a.sb("scale", [P, NB])
        inv = a.sb("inv", [P, NB])
        t = a.sb("t", [P, D])
        ge2 = a.sb("ge2", [P, D])
        ge4 = a.sb("ge4", [P, D])
        per = a.sb("per", [P, D])
        step = a.sb("step", [P, D])
        near = a.sb("near", [P, D])
        xT = a.sb("xT", [P, 2, D])
        xb = a.sb("xb", [P, 2, D])
        z = a.sb("z", [P, 2, D])
        stats = a.sb("stats", [P, 2, 6])
        mv = a.sb("mv", [P, 2, 2])
        rstd = a.sb("rstd", [P, 2, 1])
        nbias = a.sb("nbias", [P, 2, 1])
        xn = a.sb("xn", [P, 2, D])
        tr = a.psum("tr")
        yo = [a.psum(f"yo{n}") for n in range(2)]

        turns = a.sem("turns")
        w_in = a.sem("w_in")
        setup = a.sem("setup")
        wq_done = a.sem("wq_done")
        wtr_done = a.sem("wtr_done")
        wT_done = a.sem("wT_done")
        w_step = a.sem("w_step")
        x_step = a.sem("x_step")
        pool_step = a.sem("pool_step")
        x_in = [Event(a, f"x_in{n}", 1, unit=16) for n in range(2)]
        stored = [Event(a, f"stored{n}", 1, unit=16) for n in range(2)]
        xd_done = Event(a, "xd_done", 1, 1)
        tr_done = Event(a, "tr_done", 1, 1)
        xT_done = Event(a, "xT_done", 1)
        yo_done = Event(a, "yo_done", 1, 1)
        xb_done = Event(a, "xb_done", 1, 1)
        z_done = Event(a, "z_done", 1, 1)
        st_done = Event(a, "st_done", 1)
        mv_done = Event(a, "mv_done", 1)
        xn_done = Event(a, "xn_done", 1, 1)

        x_t = x.rearrange("(t p) d -> t p d", p=P)
        out_t = out.rearrange("(t p) d -> t p d", p=P)

        def passes(eng, body):
            with eng.Fori(0, TILES // 2) as m:
                body(m, 0)
                body(m, 1)
            body(TILES // 2, 0)

        block = ctx.enter_context(nc.Block())

        @block.sync
        def _(sp):
            open_all(sp, *x_in, *stored)
            sp.dma_start(ws[:, :, :], W.rearrange("(o p) k -> p o k", p=P)).then_inc(w_in, 16)
            sp.dma_start(bs[:, :], bias).then_inc(w_in, 16)

            def load(m, u):
                n = 2 * m + u
                sp.wait_ge(*xb_done.at(n, -1))
                stand(sp, turns, *xd_done.at(n, -1))
                sp.dma_start(xs[:, u, :], x_t[n]).then_inc(x_in[u].sem, 16)

            def store(m, u):
                n = 2 * m + u
                sp.wait_ge(*xn_done.at(n, 1))
                sp.dma_start(out_t[n], xn[:, u, :]).then_inc(stored[u].sem, 16)

            load(0, 0)
            load(0, 1)
            with sp.Fori(1, TILES // 2) as m:
                for u in range(2):
                    load(m, u)
                    store(m - 1, u)
            load(TILES // 2, 0)
            for n in range(TILES - 3, TILES):
                store(n // 2, n % 2)
            for u in range(2):
                sp.wait_ge(*stored[u].at((TILES + 1 - u) // 2, 0))

        @block.gpsimd
        def _(pool):
            open_all(pool, xb_done, xn_done)
            identity(pool, ident, setup, 0)
            pool.memset(half[:, :], -0.5).then_inc(setup, 1)
            pool.wait_ge(setup, 3)
            pool.wait_ge(w_in, 32)

            def add_bias(m, u):
                n = 2 * m + u
                pool.wait_ge(*x_in[u].at(m, 1))
                pool.wait_ge(*z_done.at(n, -1))
                pool.tensor_tensor(xb[:, u, :], xs[:, u, :], bs[:, :], ALU.add).then_inc(xb_done.sem, 1)

            def tile(m, u):
                n = 2 * m + u
                add_bias(m, u)
                chain = Chain(pool, turns, pool_step, n, NORM_STEPS)
                pool.wait_ge(*stored[u].at(m, 0))
                stand(pool, turns, *mv_done.at(n, 1))
                norm_rows(pool, chain, z[:, u, :], mv[:, u, :], rstd[:, u, :], nbias[:, u, :], half[:, :],
                          xn[:, u, :], xn_done.sem)
                chain.end()

            passes(pool, tile)

        @block.tensor
        def _(pe):
            open_all(pe, tr_done, yo_done)
            pe.wait_ge(setup, 3)
            for o in range(KD):
                pe.wait_ge(wq_done, o + 1)
                for k in range(KD):
                    mm = pe.transpose(yo[o][:, k * P:(k + 1) * P], wd[:, o, k * P:(k + 1) * P], ident[:, :])
                mm.then_inc(wtr_done, 1)
            pe.wait_ge(wT_done, KD)

            def tile(m, u):
                n = 2 * m + u
                pe.wait_ge(*xd_done.at(n, 1))
                pe.wait_ge(*xT_done.at(n, 0))
                for k in range(KD):
                    mm = pe.transpose(tr[:, k * P:(k + 1) * P], xd[:, u, k * P:(k + 1) * P], ident[:, :])
                mm.then_inc(tr_done.sem, 1)
                pe.wait_ge(*xT_done.at(n, 1))
                pe.wait_ge(*z_done.at(n, -1))
                for k in range(KD):
                    mm = pe.matmul(yo[u][:, 0:D], xT[:, u, k * P:(k + 1) * P], wT[:, k, :], start=(k == 0), stop=(k == KD - 1))
                mm.then_inc(yo_done.sem, 1)

            passes(pe, tile)

        @block.scalar
        def _(act):
            open_all(act, xT_done)
            for o in range(KD):
                act.wait_ge(wtr_done, o + 1)
                for k in range(KD):
                    ins = act.activation(wT[:, k, o * P:(o + 1) * P], yo[o][:, k * P:(k + 1) * P], ACT.Copy)
                ins.then_inc(wT_done, 1)

            def tile(m, u):
                n = 2 * m + u
                act.wait_ge(*tr_done.at(n, 1))
                act.wait_ge(*yo_done.at(n, -1))
                act.activation(xT[:, u, :], tr[:, 0:D], ACT.Copy).then_inc(xT_done.sem, 1)

            passes(act, tile)

        @block.vector
        def _(dve):
            open_all(dve, xd_done, z_done, st_done, mv_done)
            dve.wait_ge(w_in, 32)

            def quantise(chain, src, dst, done):
                blocks = lambda ap: ap.rearrange("p (n w) -> p n w", w=BLOCK)
                chain.then(dve.tensor_reduce(amax[:, :], blocks(src), AX.X, ALU.max, apply_absolute_value=True))
                chain.then(dve.tensor_scalar(scale[:, :], amax[:, :], 1 / 7.5, 1e-30, ALU.mult, ALU.max))
                chain.then(dve.reciprocal(inv[:, :], scale[:, :]))
                chain.then(dve.tensor_tensor(blocks(t[:, :]), blocks(src), last_bcast(inv[:, :], BLOCK), ALU.mult))
                chain.then(dve.tensor_tensor(near[:, :], t[:, :], t[:, :], ALU.mult))
                chain.then(dve.tensor_scalar(ge2[:, :], near[:, :], 4.0, None, ALU.is_ge))
                chain.then(dve.tensor_scalar(ge4[:, :], near[:, :], 16.0, None, ALU.is_ge))
                chain.then(dve.tensor_scalar(per[:, :], ge2[:, :], -4.0, 8.0, ALU.mult, ALU.add))
                chain.then(dve.scalar_tensor_tensor(per[:, :], ge4[:, :], -2.0, per[:, :], ALU.mult, ALU.add))
                chain.then(dve.tensor_scalar(step[:, :], ge2[:, :], -0.125, -0.125, ALU.mult, ALU.add))
                chain.then(dve.scalar_tensor_tensor(step[:, :], ge4[:, :], -0.25, step[:, :], ALU.mult, ALU.add))
                chain.then(dve.tensor_tensor(t[:, :], t[:, :], per[:, :], ALU.mult))
                chain.then(dve.tensor_scalar(near[:, :], t[:, :], ROUND, ROUND, ALU.add, ALU.subtract))
                chain.then(dve.tensor_tensor(t[:, :], near[:, :], t[:, :], ALU.subtract))
                chain.then(dve.scalar_tensor_tensor(t[:, :], t[:, :], 0.5, near[:, :], ALU.is_ge, ALU.subtract))
                chain.then(dve.tensor_tensor(t[:, :], t[:, :], step[:, :], ALU.mult))
                dve.tensor_tensor(blocks(dst), blocks(t[:, :]), last_bcast(scale[:, :], BLOCK), ALU.mult).then_inc(done, 1)

            for o in range(KD):
                chain = Chain(dve, turns, w_step, o, STEPS)
                quantise(chain, ws[:, o, :], wd[:, o, :], wq_done)
                chain.end()

            def quantise_x(m, u):
                n = 2 * m + u
                chain = Chain(dve, turns, x_step, n, STEPS)
                dve.wait_ge(*x_in[u].at(m, 1))
                dve.wait_ge(*tr_done.at(n, -1))
                quantise(chain, xs[:, u, :], xd[:, u, :], xd_done.sem)
                chain.end()

            def output(m, u):
                n = 2 * m + u
                dve.wait_ge(*yo_done.at(n, 1))
                dve.wait_ge(*xb_done.at(n, 1))
                dve.wait_ge(*xn_done.at(n, -1))
                dve.tensor_tensor(z[:, u, :], yo[u][:, 0:D], xb[:, u, :], ALU.add).then_inc(z_done.sem, 1)
                dve.wait_ge(*z_done.at(n, 1))
                dve.bn_stats(stats[:, u, :], z[:, u, :]).then_inc(st_done.sem, 1)
                stand(dve, turns, *st_done.at(n, 1))
                dve.bn_aggr(mv[:, u, :], stats[:, u, :]).then_inc(mv_done.sem, 1)

            quantise_x(0, 0)
            with dve.Fori(0, TILES // 2) as m:
                quantise_x(m, 1)
                output(m, 0)
                quantise_x(m + 1, 0)
                output(m, 1)
            output(TILES // 2, 0)


def normed_attention(nc, x, heads01, causal, WkqT, WvT, WuT, ln_w, ln_b, out):
    H, HD = 16, 16
    HC = P // HD
    HH = 2 * H
    with ExitStack() as ctx:
        a = Place(nc, ctx, "na")
        wkq = a.sb("wkq", [P, KD, 2 * D])
        wv = a.sb("wv", [P, KD, D])
        wu = a.sb("wu", [P, KD, D])
        lw = a.sb("lw", [P, 2 * D])
        lb = a.sb("lb", [P, 2 * D])
        cm = a.sb("cm", [S, S])
        hm = a.sb("hm", [P, HC])
        ident = a.sb("ident", [P, P])
        half = a.sb("half", [P, HH])
        xq = a.sb("xq", [S, 2, D])
        xr = a.sb("xr", [S, 2, D])
        xT = a.sb("xT", [P, KD * S])
        total = a.sb("total", [S, HH])
        mean = a.sb("mean", [S, HH])
        c = a.sb("c", [S, 2, 2 * D])
        sq = a.sb("sq", [S, 2 * D])
        total2 = a.sb("total2", [S, HH])
        rs = a.sb("rs", [S, HH])
        kT = a.sb("kT", [P, KD, S])
        qT = a.sb("qT", [P, 2, KD, S])
        kd = a.sb("kd", [P, 2, H, S])
        vm = a.sb("vm", [S, 2, H, 2 * HD])
        sm = a.sb("sm", [S, 2, 4, S])
        nb = a.sb("nb", [S, 2, 4])
        p = a.sb("p", [S, 2, 4, S])
        den = a.sb("den", [S, 2, 4])
        rec = a.sb("rec", [S, 2, 4])
        pT = a.sb("pT", [S, 2, 4 * S])
        oT = a.sb("oT", [P, 2, KD * S])
        z = a.sb("z", [S, 2, D])
        stats = a.sb("stats", [S, 2, 6])
        mv = a.sb("mv", [S, 2, 2])
        rstd = a.sb("rstd", [S, 2, 1])
        nbias = a.sb("nbias", [S, 2, 1])
        xn = a.sb("xn", [S, 2, D])
        proj = [a.psum(f"proj{n}") for n in range(2)]
        sc = [a.psum(f"sc{n}") for n in range(2)]
        tr = [a.psum(f"tr{n}") for n in range(2)]
        ov = a.psum("ov")
        yo = a.psum("yo")

        turns = a.sem("turns")
        w_in = a.sem("w_in")
        setup = a.sem("setup")
        xq_in = [Event(a, f"xq_in{n}", 1, unit=16) for n in range(2)]
        xr_in = [Event(a, f"xr_in{n}", 1, unit=16) for n in range(2)]
        stored = [Event(a, f"stored{n}", 1, unit=16) for n in range(2)]
        proj_done = Event(a, "proj_done", 4, 8)
        xT_done = Event(a, "xT_done", 1)
        sum_done = Event(a, "sum_done", 1)
        mean_done = Event(a, "mean_done", 1)
        c_done = Event(a, "c_done", 1)
        sq_done = Event(a, "sq_done", 1)
        sum2_done = Event(a, "sum2_done", 1)
        rs_done = Event(a, "rs_done", 2)
        cn_done = Event(a, "cn_done", 1)
        ln_done = Event(a, "ln_done", 2)
        v_done = Event(a, "v_done", 1)
        qk_done = Event(a, "qk_done", 1)
        kd_done = Event(a, "kd_done", KD)
        sc_done = Event(a, "sc_done", 4)
        mx_done = Event(a, "mx_done", H, 4)
        exp_done = Event(a, "exp_done", H, 4)
        rec_done = Event(a, "rec_done", 4)
        pn_done = Event(a, "pn_done", 4)
        tr_done = Event(a, "tr_done", 4, 1)
        ca_done = Event(a, "ca_done", 2)
        cd_done = Event(a, "cd_done", 2)
        ov_done = Event(a, "ov_done", 4, 4)
        oT_done = Event(a, "oT_done", 1)
        yo_done = Event(a, "yo_done", 1, 1)
        z_done = Event(a, "z_done", 1, 1)
        st_done = Event(a, "st_done", 1)
        mv_done = Event(a, "mv_done", 1)
        xn_done = Event(a, "xn_done", 1, 2)
        pool_step = a.sem("pool_step")
        LOADS = 7

        x_s = x.rearrange("(b s) d -> b s d", s=S)
        out_s = out.rearrange("(b s) d -> b s d", s=S)

        def prev(m, u):
            return (m, 0) if u else (m - 1, 1)

        def passes(eng, body):
            body(0, 0, behind=False)
            body(0, 1)
            with eng.Fori(1, B // 2 - 1) as m:
                body(m, 0)
                body(m, 1)
            body(B // 2 - 1, 0, beyond=False)
            body(B // 2 - 1, 1, ahead=False, beyond=False)
            body(B // 2, 0, here=False, ahead=False, beyond=False)

        block = ctx.enter_context(nc.Block())

        @block.sync
        def _(sp):
            open_all(sp, *xq_in, *xr_in, *stored)
            sp.dma_start(wkq[:, :, :], WkqT.rearrange("(k p) n -> p k n", p=P)).then_inc(w_in, 16)
            sp.dma_start(wv[:, :, :], WvT.rearrange("(k p) n -> p k n", p=P)).then_inc(w_in, 16)
            sp.dma_start(wu[:, :, :], WuT.rearrange("(k p) n -> p k n", p=P)).then_inc(w_in, 16)
            sp.dma_start(lw[:, :], ln_w).then_inc(w_in, 16)
            sp.dma_start(lb[:, :], ln_b).then_inc(w_in, 16)
            sp.dma_start(hm[:, :], heads01).then_inc(w_in, 16)
            sp.dma_start(cm[:, :], causal).then_inc(w_in, 16)

            def load(m, u):
                n = 2 * m + u
                sp.wait_ge(*proj_done.at(n, -7))
                sp.dma_start(xq[:, u, :], x_s[n]).then_inc(xq_in[u].sem, 16)

            def load_residual(m, u):
                n = 2 * m + u
                sp.wait_ge(*z_done.at(n, -1))
                sp.dma_start(xr[:, u, :], x_s[n]).then_inc(xr_in[u].sem, 16)

            def store(m, u):
                n = 2 * m + u
                sp.wait_ge(*xn_done.at(n, 1))
                sp.dma_start(out_s[n], xn[:, u, :]).then_inc(stored[u].sem, 16)

            LAST = B // 2 - 1
            for m in range(2):
                for u in range(2):
                    load(m, u)
            load_residual(0, 0)
            load_residual(0, 1)
            with sp.Fori(2, LAST + 1) as m:
                for u in range(2):
                    load(m, u)
                    store(m - 2, u)
                    load_residual(m - 1, u)
            for u in range(2):
                store(LAST - 1, u)
                load_residual(LAST, u)
            store(LAST, 0)
            store(LAST, 1)
            for u in range(2):
                sp.wait_ge(*stored[u].at(B // 2, 0))

        @block.gpsimd
        def _(pool):
            open_all(pool, rs_done, ln_done, kd_done, xn_done)
            identity(pool, ident, setup, 0)
            pool.memset(half[:, :], -0.5).then_inc(setup, 1)
            pool.memset(vm[:, :, :, :], 0.0).then_inc(setup, 1)
            pool.wait_ge(setup, 4)
            pool.wait_ge(w_in, 16 * LOADS)

            def root(m, u):
                n = 2 * m + u
                stand(pool, turns, *sum2_done.at(n, 1))
                pool.tensor_scalar(rs[:, :], total2[:, :], 1 / HD, LN_EPS, ALU.mult, ALU.add).then_inc(rs_done.sem, 1)
                pool.wait_ge(*rs_done.at(n, 1))
                pool.tensor_tensor(rs[:, :], rs[:, :], half[0:S, :], ALU.pow).then_inc(rs_done.sem, 1)

            def affine(m, u):
                n = 2 * m + u
                pool.wait_ge(*cn_done.at(n, 1))
                pool.tensor_tensor(c[:, u, :], c[:, u, :], lw[0:S, :], ALU.mult).then_inc(ln_done.sem, 1)
                pool.wait_ge(*ln_done.at(n, 1))
                pool.tensor_tensor(c[:, u, :], c[:, u, :], lb[0:S, :], ALU.add).then_inc(ln_done.sem, 1)

            def part_heads(m, u):
                n = 2 * m + u
                pool.wait_ge(*qk_done.at(n, 1))
                for k in range(KD):
                    pool.tensor_tensor(kd[:, u, HC * k:HC * k + HC, :], mid_bcast(kT[:, k, :], HC),
                                       last_bcast(hm[:, :], S), ALU.mult).then_inc(kd_done.sem, 1)

            def norm(m, u):
                n = 2 * m + u
                chain = Chain(pool, turns, pool_step, n, NORM_STEPS)
                pool.wait_ge(*stored[u].at(m, 0))
                stand(pool, turns, *mv_done.at(n, 1))
                norm_rows(pool, chain, z[:, u, :], mv[:, u, :], rstd[:, u, :], nbias[:, u, :], half[0:S, 0:1],
                          xn[:, u, :], xn_done.sem)
                chain.end()

            def sequence(m, u, behind=True, here=True, ahead=True, beyond=True):
                following = (m, 1) if u == 0 else (m + 1, 0)
                if ahead:
                    affine(*following)
                    part_heads(*following)
                if beyond:
                    root(m + 1, u)
                if behind:
                    norm(*prev(m, u))

            root(0, 0)
            affine(0, 0)
            part_heads(0, 0)
            root(0, 1)
            passes(pool, sequence)

        @block.tensor
        def _(pe):
            open_all(pe, proj_done, sc_done, tr_done, ov_done, yo_done)
            pe.wait_ge(w_in, 16 * LOADS)
            pe.wait_ge(setup, 4)

            def turn_x(m, u):
                n = 2 * m + u
                pe.wait_ge(*xq_in[u].at(m, 1))
                pe.wait_ge(*v_done.at(n, 0))
                for k in range(KD):
                    mm = pe.transpose(proj[0][:, k * S:(k + 1) * S], xq[:, u, k * P:(k + 1) * P], ident[0:S, 0:S])
                mm.then_inc(proj_done.sem, 1)

            def project(m, u):
                n = 2 * m + u
                pe.wait_ge(*xT_done.at(n, 1))
                pe.wait_ge(*qk_done.at(n, 0))
                for k in range(KD):
                    mm = pe.matmul(proj[1][0:S, :], xT[:, k * S:(k + 1) * S], wkq[:, k, :], start=(k == 0), stop=(k == KD - 1))
                mm.then_inc(proj_done.sem, 1)
                for k in range(KD):
                    mm = pe.matmul(proj[0][0:S, 0:D], xT[:, k * S:(k + 1) * S], wv[:, k, :], start=(k == 0), stop=(k == KD - 1))
                mm.then_inc(proj_done.sem, 1)

            def turn_kq(m, u):
                n = 2 * m + u
                pe.wait_ge(*ln_done.at(n, 2))
                for k in range(2 * KD):
                    mm = pe.transpose(proj[1][:, k * S:(k + 1) * S], c[:, u, k * P:(k + 1) * P], ident[0:S, 0:S])
                mm.then_inc(proj_done.sem, 1)

            def scores(m, u, r):
                n = 2 * m + u
                pe.wait_ge(*kd_done.at(n, r // 2 + 1))
                pe.wait_ge(*mx_done.at(n, 4 * r - 4))
                pe.matmul(sc[r % 2][0:S, 0:4 * S], qT[:, u, r // 2, :], kd[:, u, 4 * r:4 * r + 4, :],
                          start=True, stop=True).then_inc(sc_done.sem, 1)

            def turn(m, u, r):
                n = 2 * m + u
                pe.wait_ge(*pn_done.at(n, r + 1))
                pe.wait_ge(*(cd_done if r % 2 else ca_done).at(n, r // 2))
                for j in range(4):
                    mm = pe.transpose(tr[r % 2][0:S, j * S:(j + 1) * S], p[:, r % 2, j, :], ident[0:S, 0:S])
                mm.then_inc(tr_done.sem, 1)

            def values(m, u, r):
                n = 2 * m + u
                if r == 0:
                    pe.wait_ge(*v_done.at(n, 1))
                    pe.wait_ge(*oT_done.at(n, 0))
                pe.wait_ge(*(cd_done if r % 2 else ca_done).at(n, r // 2 + 1))
                for j in range(4):
                    h = 4 * r + j
                    g = h // 2
                    mm = pe.matmul(ov[32 * (g % 4):32 * (g % 4) + 32, (g // 4) * S:(g // 4 + 1) * S],
                                   vm[:, u, h, :], pT[:, r % 2, j * S:(j + 1) * S], start=(j % 2 == 0), stop=(j % 2 == 1))
                mm.then_inc(ov_done.sem, 1)

            def project_out(m, u):
                n = 2 * m + u
                pe.wait_ge(*oT_done.at(n, 1))
                pe.wait_ge(*z_done.at(n, 0))
                for k in range(KD):
                    mm = pe.matmul(yo[0:S, 0:D], oT[:, u, k * S:(k + 1) * S], wu[:, k, :], start=(k == 0), stop=(k == KD - 1))
                mm.then_inc(yo_done.sem, 1)

            def sequence(m, u, behind=True, here=True, ahead=True, beyond=True):
                following = (m, 1) if u == 0 else (m + 1, 0)
                for r in range(4 if here else 2):
                    if here:
                        scores(m, u, r)
                    if r >= 1:
                        if here:
                            turn(m, u, r - 1)
                    elif behind:
                        turn(*prev(m, u), 3)
                    if r >= 2:
                        values(m, u, r - 2)
                    elif behind:
                        values(*prev(m, u), r + 2)
                    if ahead and r == 2:
                        turn_kq(*following)
                    if beyond and r == 2:
                        turn_x(m + 1, u)
                    if beyond and r == 3:
                        project(m + 1, u)
                    if behind and r == (2 if here else 1):
                        project_out(*prev(m, u))

            turn_x(0, 0)
            project(0, 0)
            turn_kq(0, 0)
            turn_x(0, 1)
            project(0, 1)
            passes(pe, sequence)

        @block.scalar
        def _(act):
            open_all(act, xT_done, v_done, sq_done, qk_done, exp_done, ca_done, oT_done)
            act.wait_ge(setup, 4)

            def copy_x(m, u):
                n = 2 * m + u
                act.wait_ge(*proj_done.at(n, 1))
                act.activation(xT[:, :], proj[0][:, 0:KD * S], ACT.Copy).then_inc(xT_done.sem, 1)

            def copy_v(m, u):
                n = 2 * m + u
                act.wait_ge(*proj_done.at(n, 3))
                act.wait_ge(*ov_done.at(n, -4))
                bank = proj[0][0:S, 0:D].rearrange("p (g e d) -> p g e d", e=2, d=HD)
                for e in range(2):
                    ins = act.activation(vm[:, u, e:H:2, HD * e:HD * e + HD], bank[:, :, e, :], ACT.Copy)
                ins.then_inc(v_done.sem, 1)

            def square(m, u):
                n = 2 * m + u
                act.wait_ge(*c_done.at(n, 1))
                act.activation(sq[:, :], c[:, u, :], ACT.Square).then_inc(sq_done.sem, 1)

            def copy_kq(m, u):
                n = 2 * m + u
                act.wait_ge(*proj_done.at(n, 4))
                act.wait_ge(*kd_done.at(n, 0))
                act.activation(kT[:, :, :].rearrange("p k s -> p (k s)"), proj[1][:, 0:KD * S], ACT.Copy)
                act.activation(qT[:, u, :, :].rearrange("p k s -> p (k s)"), proj[1][:, KD * S:2 * KD * S],
                               ACT.Copy).then_inc(qk_done.sem, 1)

            def exps(m, u, r):
                n = 2 * m + u
                act.wait_ge(*tr_done.at(n, r - 1))
                for j in range(4):
                    act.wait_ge(*mx_done.at(n, 4 * r + j + 1))
                    act.activation(p[:, r % 2, j, :], sm[:, r % 2, j, :], ACT.Exp, bias=nb[:, r % 2, j:j + 1], scale=-1.0,
                                   accum_out=den[:, r % 2, j:j + 1]).then_inc(exp_done.sem, 1)

            def copy_turned(m, u, r):
                n = 2 * m + u
                if r % 2 == 0:
                    act.wait_ge(*ov_done.at(n, r - 1))
                    act.wait_ge(*tr_done.at(n, r + 1))
                    act.activation(pT[:, 0, :], tr[0][0:S, 0:4 * S], ACT.Copy).then_inc(ca_done.sem, 1)

            def copy_out(m, u):
                n = 2 * m + u
                act.wait_ge(*ov_done.at(n, 4))
                act.wait_ge(*yo_done.at(n, -1))
                act.activation(oT[:, u, :], ov[:, 0:KD * S], ACT.Copy).then_inc(oT_done.sem, 1)

            def sequence(m, u, behind=True, here=True, ahead=True, beyond=True):
                following = (m, 1) if u == 0 else (m + 1, 0)
                for r in range(4 if here else 2):
                    if beyond and r == 3:
                        copy_x(m + 1, u)
                    if here:
                        exps(m, u, r)
                    if r >= 1:
                        if here:
                            copy_turned(m, u, r - 1)
                    elif behind:
                        copy_turned(*prev(m, u), 3)
                    if ahead:
                        if r == 1:
                            copy_v(*following)
                        if r == 2:
                            copy_kq(*following)
                    if beyond and r == 3:
                        square(m + 1, u)
                    if behind and r == 1:
                        copy_out(*prev(m, u))

            copy_x(0, 0)
            copy_v(0, 0)
            square(0, 0)
            copy_kq(0, 0)
            copy_x(0, 1)
            square(0, 1)
            passes(act, sequence)

        @block.vector
        def _(dve):
            open_all(dve, sum_done, mean_done, c_done, sum2_done, cn_done, mx_done, cd_done, rec_done, pn_done, z_done,
                     st_done, mv_done)
            dve.wait_ge(w_in, 16 * LOADS)
            heads = lambda ap: ap.rearrange("p (h d) -> p h d", d=HD)

            def centre(m, u):
                n = 2 * m + u
                dve.wait_ge(*proj_done.at(n, 2))
                dve.tensor_reduce(total[:, :], heads(proj[1][0:S, :]), AX.X, ALU.add).then_inc(sum_done.sem, 1)
                dve.wait_ge(*sum_done.at(n, 1))
                dve.tensor_scalar(mean[:, :], total[:, :], 1 / HD, None, ALU.mult).then_inc(mean_done.sem, 1)
                dve.wait_ge(*mean_done.at(n, 1))
                dve.tensor_tensor(heads(c[:, u, :]), heads(proj[1][0:S, :]), last_bcast(mean[:, :], HD),
                                  ALU.subtract).then_inc(c_done.sem, 1)

            def sum_squares(m, u):
                n = 2 * m + u
                dve.wait_ge(*sq_done.at(n, 1))
                dve.tensor_reduce(total2[:, :], heads(sq[:, :]), AX.X, ALU.add).then_inc(sum2_done.sem, 1)

            def scale(m, u):
                n = 2 * m + u
                dve.wait_ge(*rs_done.at(n, 2))
                dve.tensor_tensor(heads(c[:, u, :]), heads(c[:, u, :]), last_bcast(rs[:, :], HD),
                                  ALU.mult).then_inc(cn_done.sem, 1)

            def maxima(m, u, r):
                n = 2 * m + u
                dve.wait_ge(*exp_done.at(n, 4 * r - 4))
                stand(dve, turns, *sc_done.at(n, r + 1))
                for j in range(4):
                    dve.tensor_tensor_reduce(sm[:, r % 2, j, :], sc[r % 2][0:S, j * S:(j + 1) * S], cm[:, :], -1 / 4, 3e38,
                                             ALU.add, ALU.min, nb[:, r % 2, j:j + 1]).then_inc(mx_done.sem, 1)

            def copy_turned(m, u, r):
                n = 2 * m + u
                if r % 2:
                    dve.wait_ge(*ov_done.at(n, r - 1))
                    dve.wait_ge(*tr_done.at(n, r + 1))
                    dve.tensor_copy(pT[:, 1, :], tr[1][0:S, 0:4 * S]).then_inc(cd_done.sem, 1)

            def probabilities(m, u, r):
                n = 2 * m + u
                dve.wait_ge(*exp_done.at(n, 4 * r + 4))
                dve.reciprocal(rec[:, r % 2, :], den[:, r % 2, :]).then_inc(rec_done.sem, 1)
                dve.wait_ge(*rec_done.at(n, r + 1))
                dve.tensor_tensor(p[:, r % 2, :, :], p[:, r % 2, :, :], last_bcast(rec[:, r % 2, :], S),
                                  ALU.mult).then_inc(pn_done.sem, 1)

            def output(m, u):
                n = 2 * m + u
                dve.wait_ge(*yo_done.at(n, 1))
                dve.wait_ge(*xr_in[u].at(m, 1))
                dve.wait_ge(*xn_done.at(n, -1))
                dve.tensor_tensor(z[:, u, :], yo[0:S, 0:D], xr[:, u, :], ALU.add).then_inc(z_done.sem, 1)
                dve.wait_ge(*z_done.at(n, 1))
                dve.bn_stats(stats[:, u, :], z[:, u, :]).then_inc(st_done.sem, 1)
                stand(dve, turns, *st_done.at(n, 1))
                dve.bn_aggr(mv[:, u, :], stats[:, u, :]).then_inc(mv_done.sem, 1)

            def sequence(m, u, behind=True, here=True, ahead=True, beyond=True):
                following = (m, 1) if u == 0 else (m + 1, 0)
                for r in range(4 if here else 2):
                    if here:
                        maxima(m, u, r)
                    if r >= 1:
                        if here:
                            copy_turned(m, u, r - 1)
                    elif behind:
                        copy_turned(*prev(m, u), 3)
                    if ahead and r == 1:
                        scale(*following)
                    if beyond and r == 3:
                        centre(m + 1, u)
                    if here:
                        probabilities(m, u, r)
                    if beyond and r == 3:
                        sum_squares(m + 1, u)
                    if behind and r == (3 if here else 1):
                        output(*prev(m, u))

            centre(0, 0)
            sum_squares(0, 0)
            scale(0, 0)
            centre(0, 1)
            sum_squares(0, 1)
            passes(dve, sequence)


def sparse_attention(nc, x, cT, heads4, Wq, bq, Wk, bk, Wv, bv, Wo, bo, out, sum_max, newton, tag):
    H, HD = 16, 16
    HC = P // HD
    NK = len(KEYS)
    HALF = H // 2
    TURNED = (2, 4, 7)
    STEP_AT = 2
    SC = 3
    PARTS = [(0, 90), (90, 90), (180, 90), (270, 91)]
    NC = 8 * len(PARTS)
    with ExitStack() as ctx:
        a = Place(nc, ctx, tag)
        wq = a.sb("wq", [P, KD, D])
        wk = a.sb("wk", [P, KD, D])
        wv = a.sb("wv", [P, KD, D])
        wo = a.sb("wo", [P, KD, D])
        bqs = a.sb("bqs", [P, KD])
        bks = a.sb("bks", [P, KD])
        bvs = a.sb("bvs", [P, D])
        bos = a.sb("bos", [P, D])
        hm = a.sb("hm", [P, HC])
        ident = a.sb("ident", [P, P])
        half = a.sb("half", [P, 1])
        cTs = a.sb("cTs", [P, 2, KD, S2])
        xq = a.sb("xq", [S, 2, D])
        xr = a.sb("xr", [S, 2, D])
        xT = a.sb("xT", [P, KD * S])
        qs = a.sb("qs", [P, KD, S])
        qm = a.sb("qm", [P, 2, H, S])
        kT = a.sb("kT", [P, 2, KD, S2])
        vm = a.sb("vm", [P, 2, NK, H, 2 * HD])
        zs = a.sb("zs", [S, 2, H, S2])
        cand = a.sb("cand", [S, H, NC])
        high = a.sb("high", [S, H])
        over = a.sb("over", [S, H, NC])
        above = a.sb("above", [S, H, NC])
        csum = a.sb("csum", [S, H])
        ccount = a.sb("ccount", [S, H])
        nt = a.sb("nt", [S, 2, H])
        rec = a.sb("rec", [S, H])
        gain = a.sb("gain", [S, H])
        total = a.sb("total", [S, H])
        count = a.sb("count", [S, H])
        spare_a = a.sb("spare_a", [S, 2, HALF, S2])
        spare_d = a.sb("spare_d", [S, 2, HALF, S2], BF16)
        den = a.sb("den", [S, 2, H])
        worst = a.sb("worst", [S, H])
        top = a.sb("top", [S, 1])
        pT = a.sb("pT", [P, 2, NK, 4 * S])
        oT = a.sb("oT", [P, 2, KD * S])
        xb = a.sb("xb", [S, 2, D])
        z = a.sb("z", [S, 2, D])
        stats = a.sb("stats", [S, 2, 6])
        mv = a.sb("mv", [S, 2, 2])
        rstd = a.sb("rstd", [S, 2, 1])
        nbias = a.sb("nbias", [S, 2, 1])
        xn = a.sb("xn", [S, 2, D])
        proj = [a.psum(f"proj{n}") for n in range(2)]
        sc = [a.psum(f"sc{n}") for n in range(SC)]
        tr = [a.psum(f"tr{n}") for n in range(2)]
        oy = a.psum("oy")
        ov, yo = oy[:, 0:KD * S], oy[:, D:2 * D]

        turns = a.sem("turns")
        w_in = a.sem("w_in")
        setup = a.sem("setup")
        xq_in = [Event(a, f"xq_in{n}", 1, unit=16) for n in range(2)]
        cT_in = [Event(a, f"cT_in{n}", 1, unit=16) for n in range(2)]
        xr_in = [Event(a, f"xr_in{n}", 1, unit=16) for n in range(2)]
        stored = [Event(a, f"stored{n}", 1, unit=16) for n in range(2)]
        proj_done = Event(a, "proj_done", 8, 16)
        qk_done = Event(a, "qk_done", 5)
        v_done = Event(a, "v_done", 3, 1)
        qm_done = Event(a, "qm_done", 1)
        sc_done = Event(a, "sc_done", H)
        cand_done = Event(a, "cand_done", H)
        high_done = Event(a, "high_done", H)
        z_in = Event(a, "z_in", H, SC)
        start_done = Event(a, "start_done", 2)
        t_done = Event(a, "t_done", 2 * newton)
        total_done = Event(a, "total_done", 2 * newton, 1)
        count_done = Event(a, "count_done", 2 * newton, 1)
        p_done = Event(a, "p_done", 2)
        tr_done = Event(a, "tr_done", 4 * NK, 8 * NK)
        ca_done = Event(a, "ca_done", 2 * NK)
        cd_done = Event(a, "cd_done", 2 * NK)
        ov_done = Event(a, "ov_done", 4, 8)
        oT_done = Event(a, "oT_done", 1)
        yo_done = Event(a, "yo_done", 1, 1)
        xb_done = Event(a, "xb_done", 1, 2)
        z_done = Event(a, "z_done", 1, 1)
        st_done = Event(a, "st_done", 1)
        mv_done = Event(a, "mv_done", 1)
        xn_done = Event(a, "xn_done", 1, 2)
        worst_done = Event(a, "worst_done", 1, 1)
        pool_step = a.sem("pool_step")
        cand_step = a.sem("cand_step")
        newton_step = a.sem("newton_step")
        top_step = a.sem("top_step")
        top_out = a.sem("top_out")
        cleared = a.sem("cleared")
        LOADS = 9
        NEWTON_STEPS = 2 * 2 * newton
        START = 12

        x_s = x.rearrange("(b s) d -> b s d", s=S)
        out_s = out.rearrange("(b s) d -> b s d", s=S)
        cT_s = cT.rearrange("b (k p) n -> b p k n", p=P)

        def prev(m, u):
            return (m, 0) if u else (m - 1, 1)

        block = ctx.enter_context(nc.Block())

        @block.sync
        def _(sp):
            open_all(sp, *xq_in, *cT_in, *xr_in, *stored)
            sp.dma_start(wq[:, :, :], Wq.rearrange("(k p) n -> p k n", p=P)).then_inc(w_in, 16)
            sp.dma_start(wk[:, :, :], Wk.rearrange("(k p) n -> p k n", p=P)).then_inc(w_in, 16)
            sp.dma_start(wv[:, :, :], Wv.rearrange("(k p) n -> p k n", p=P)).then_inc(w_in, 16)
            sp.dma_start(wo[:, :, :], Wo.rearrange("(k p) n -> p k n", p=P)).then_inc(w_in, 16)
            sp.dma_start(bos[:, :], bo).then_inc(w_in, 16)
            sp.dma_start(bqs[:, :], bq).then_inc(w_in, 16)
            sp.dma_start(bks[:, :], bk).then_inc(w_in, 16)
            sp.dma_start(bvs[:, :], bv).then_inc(w_in, 16)
            sp.dma_start(hm[:, :], heads4).then_inc(w_in, 16)

            def load(m, u):
                n = 2 * m + u
                sp.wait_ge(*proj_done.at(n, -15))
                sp.dma_start(xq[:, u, :], x_s[n]).then_inc(xq_in[u].sem, 16)
                sp.wait_ge(*proj_done.at(n, -8))
                sp.dma_start(cTs[:, u, :, :], cT_s[n]).then_inc(cT_in[u].sem, 16)

            def load_residual(m, u):
                n = 2 * m + u
                sp.wait_ge(*xb_done.at(n, -1))
                sp.dma_start(xr[:, u, :], x_s[n]).then_inc(xr_in[u].sem, 16)

            def store(m, u):
                n = 2 * m + u
                sp.wait_ge(*xn_done.at(n, 1))
                sp.dma_start(out_s[n], xn[:, u, :]).then_inc(stored[u].sem, 16)

            load(0, 0)
            load(0, 1)
            load_residual(0, 0)
            load_residual(0, 1)
            with sp.Fori(1, B // 2) as m:
                for u in range(2):
                    load(m, u)
                    store(m - 1, u)
                    load_residual(m, u)
            store(B // 2 - 1, 0)
            store(B // 2 - 1, 1)
            sp.wait_ge(top_step, 1)
            sp.dma_start(sum_max, top[:, :]).then_inc(top_out, 16)
            for u in range(2):
                sp.wait_ge(*stored[u].at(B // 2, 0))
            sp.wait_ge(top_out, 16)

        def passes(eng, body):
            body(0, 0, behind=False)
            body(0, 1)
            with eng.Fori(1, B // 2 - 1) as m:
                body(m, 0)
                body(m, 1)
            body(B // 2 - 1, 0)
            body(B // 2 - 1, 1, ahead=False)
            body(B // 2, 0, here=False, ahead=False)

        @block.gpsimd
        def _(pool):
            open_all(pool, qm_done, xb_done, xn_done)
            identity(pool, ident, setup, 0)
            pool.memset(half[:, :], -0.5).then_inc(setup, 1)
            pool.memset(vm[:, :, :, :, :], 0.0).then_inc(setup, 1)
            pool.wait_ge(setup, 4)
            pool.wait_ge(w_in, 16 * LOADS)

            def part_heads(m, u):
                n = 2 * m + u
                pool.wait_ge(*qk_done.at(n, 3))
                for k in range(KD):
                    ins = pool.tensor_tensor(qm[:, u, HC * k:HC * k + HC, :], mid_bcast(qs[:, k, :], HC),
                                             last_bcast(hm[:, :], S), ALU.mult)
                ins.then_inc(qm_done.sem, 1)

            def add_bias(m, u):
                n = 2 * m + u
                pool.wait_ge(*xr_in[u].at(m, 1))
                pool.wait_ge(*z_done.at(n, -1))
                pool.tensor_tensor(xb[:, u, :], xr[:, u, :], bos[0:S, :], ALU.add).then_inc(xb_done.sem, 1)

            def norm(m, u):
                n = 2 * m + u
                chain = Chain(pool, turns, pool_step, n, NORM_STEPS)
                pool.wait_ge(*stored[u].at(m, 0))
                stand(pool, turns, *mv_done.at(n, 1))
                norm_rows(pool, chain, z[:, u, :], mv[:, u, :], rstd[:, u, :], nbias[:, u, :], half[0:S, :],
                          xn[:, u, :], xn_done.sem)
                chain.end()

            def sequence(m, u, behind=True, here=True, ahead=True):
                if ahead:
                    part_heads(*((m, 1) if u == 0 else (m + 1, 0)))
                if here:
                    add_bias(m, u)
                if behind:
                    norm(*prev(m, u))

            part_heads(0, 0)
            passes(pool, sequence)

        @block.tensor
        def _(pe):
            open_all(pe, proj_done, sc_done, tr_done, ov_done, yo_done)
            pe.wait_ge(w_in, 16 * LOADS)
            pe.wait_ge(setup, 4)

            def bank_free(n, f):
                if f < 2:
                    pe.wait_ge(*v_done.at(n, f - 1))
                elif f < 7:
                    pe.wait_ge(*qk_done.at(n, f - 1))
                else:
                    pe.wait_ge(*v_done.at(n, 1))

            def turn_x(m, u):
                n = 2 * m + u
                pe.wait_ge(*xq_in[u].at(m, 1))
                bank_free(n, 0)
                for k in range(KD):
                    mm = pe.transpose(proj[0][:, k * S:(k + 1) * S], xq[:, u, k * P:(k + 1) * P], ident[0:S, 0:S])
                mm.then_inc(proj_done.sem, 1)

            def project_q(m, u):
                n = 2 * m + u
                pe.wait_ge(*qk_done.at(n, 1))
                for c in range(KD):
                    bank_free(n, 1 + c)
                    for k in range(KD):
                        mm = pe.matmul(proj[(1 + c) % 2][:, 0:S], wq[:, k, c * P:(c + 1) * P], xT[:, k * S:(k + 1) * S],
                                       start=(k == 0), stop=(k == KD - 1))
                    mm.then_inc(proj_done.sem, 1)

            def project_k(m, u):
                n = 2 * m + u
                pe.wait_ge(*cT_in[u].at(m, 1))
                for c in range(KD):
                    bank_free(n, 3 + c)
                    for k in range(KD):
                        mm = pe.matmul(proj[(3 + c) % 2][:, 0:S2], wk[:, k, c * P:(c + 1) * P], cTs[:, u, k, :],
                                       start=(k == 0), stop=(k == KD - 1))
                    mm.then_inc(proj_done.sem, 1)

            def project_v(m, u):
                n = 2 * m + u
                for t, (k0, kn) in enumerate(KEYS):
                    bank_free(n, 5 + t)
                    for k in range(KD):
                        mm = pe.matmul(proj[(5 + t) % 2][0:kn, 0:D], cTs[:, u, k, k0:k0 + kn], wv[:, k, :],
                                       start=(k == 0), stop=(k == KD - 1))
                    mm.then_inc(proj_done.sem, 1)

            def scores(m, u, h):
                n = 2 * m + u
                if h == 0:
                    pe.wait_ge(*qm_done.at(n, 1))
                    pe.wait_ge(*qk_done.at(n, 5))
                pe.wait_ge(*z_in.at(n, max(h - SC + 1, 0)))
                pe.matmul(sc[h % SC][0:S, 0:S2], qm[:, u, h, :], kT[:, u, h // HC, :],
                          start=True, stop=True).then_inc(sc_done.sem, 1)

            def turn(m, u, r, t):
                n = 2 * m + u
                f = NK * r + t
                if t == 0:
                    pe.wait_ge(*p_done.at(n, r // 2 + 1))
                pe.wait_ge(*(cd_done if f % 2 else ca_done).at(n, f // 2))
                k0, kn = KEYS[t]
                for j in range(4):
                    mm = pe.transpose(tr[f % 2][0:kn, j * S:(j + 1) * S], zs[:, u, 4 * r + j, k0:k0 + kn], ident[0:S, 0:S])
                mm.then_inc(tr_done.sem, 1)

            def values(m, u, r, t):
                n = 2 * m + u
                f = NK * r + t
                if r == 0 and t == 0:
                    pe.wait_ge(*v_done.at(n, 3))
                    pe.wait_ge(*oT_done.at(n, 0))
                pe.wait_ge(*(cd_done if f % 2 else ca_done).at(n, f // 2 + 1))
                kn = KEYS[t][1]
                for j in range(4):
                    h = 4 * r + j
                    g = h // 2
                    mm = pe.matmul(ov[32 * (g % 4):32 * (g % 4) + 32, (g // 4) * S:(g // 4 + 1) * S],
                                   vm[0:kn, u, t, h, :], pT[0:kn, r % 2, t, j * S:(j + 1) * S],
                                   start=(t == 0 and j % 2 == 0), stop=(t == NK - 1 and j % 2 == 1))
                if t == NK - 1:
                    mm.then_inc(ov_done.sem, 1)

            def project_out(m, u):
                n = 2 * m + u
                pe.wait_ge(*oT_done.at(n, 1))
                pe.wait_ge(*z_done.at(n, 0))
                for k in range(KD):
                    mm = pe.matmul(yo[0:S, 0:D], oT[:, u, k * S:(k + 1) * S], wo[:, k, :], start=(k == 0), stop=(k == KD - 1))
                mm.then_inc(yo_done.sem, 1)

            def sequence(m, u, behind=True, here=True, ahead=True):
                following = (m, 1) if u == 0 else (m + 1, 0)
                for r in range(5):
                    if ahead and r < 3:
                        (turn_x, project_q, project_k)[r](*following)
                    for t in range(NK):
                        if ahead and r >= 2:
                            scores(*following, 4 * (r - 2) + t)
                        if behind and r < 4:
                            turn(*prev(m, u), r, t)
                        if behind and r >= 1:
                            values(*prev(m, u), r - 1, t)
                    if ahead and r >= 2:
                        scores(*following, 4 * (r - 2) + 3)
                if ahead:
                    project_v(*following)
                    for h in range(12, 16):
                        scores(*following, h)
                if behind:
                    project_out(*prev(m, u))

            turn_x(0, 0)
            project_q(0, 0)
            project_k(0, 0)
            for h in range(H):
                if h == 12:
                    project_v(0, 0)
                scores(0, 0, h)
            passes(pe, sequence)

        @block.scalar
        def _(act):
            open_all(act, qk_done, z_in, total_done, p_done, ca_done, oT_done)
            act.wait_ge(w_in, 16 * LOADS)
            act.wait_ge(setup, 4)

            def copy_proj(m, u, f):
                n = 2 * m + u
                bank = proj[f % 2]
                act.wait_ge(*proj_done.at(n, f + 1))
                if f == 0:
                    ins = act.activation(xT[:, :], bank[:, 0:KD * S], ACT.Copy)
                elif f < 3:
                    if f == 1:
                        act.wait_ge(*qm_done.at(n, 0))
                    ins = act.activation(qs[:, f - 1, :], bank[:, 0:S], ACT.Identity, bias=bqs[:, f - 1:f])
                else:
                    ins = act.activation(kT[:, u, f - 3, :], bank[:, 0:S2], ACT.Identity, bias=bks[:, f - 3:f - 2])
                ins.then_inc(qk_done.sem, 1)

            def copy_scores(m, u, h):
                n = 2 * m + u
                if h % 4 == 0:
                    act.wait_ge(*tr_done.at(n, NK * (h // 4 + 1) - 8 * NK))
                act.wait_ge(*high_done.at(n, h + 1))
                act.activation(zs[:, u, h, :], sc[h % SC][0:S, 0:S2], ACT.Identity,
                               bias=high[:, h:h + 1], scale=-1.0).then_inc(z_in.sem, 1)

            def sums(m, u, s, here, copy, turned):
                n = 2 * m + u
                e = s % 2
                if not here:
                    pass
                elif s < 2:
                    act.wait_ge(*start_done.at(n, e + 1))
                    act.wait_ge(*z_in.at(n, HALF * e + HALF))
                else:
                    act.wait_ge(*t_done.at(n, s - 1))
                if here:
                    act.wait_ge(*total_done.at(n, s - 1))
                for j in range(HALF):
                    h = HALF * e + j
                    if here:
                        ins = act.activation(spare_a[:, e, j, :], zs[:, u, h, :], ACT.Relu, bias=nt[:, u, h:h + 1],
                                             scale=-1.0, accum_out=total[:, h:h + 1])
                        if j == HALF - 1:
                            ins.then_inc(total_done.sem, 1)
                    if j % 2 and copy and 2 <= s < 6:
                        copy_scores(*copy, 4 * (s - 2) + j // 2)
                    if j in TURNED and turned and s < 4:
                        copy_turned(*turned, s, TURNED.index(j))

            def probabilities(m, u, e):
                n = 2 * m + u
                act.wait_ge(*t_done.at(n, 2 * newton - 1 + e))
                if e == 0:
                    act.wait_ge(*worst_done.at(n, -1))
                for h in range(HALF * e, HALF * e + HALF):
                    ins = act.activation(zs[:, u, h, :], zs[:, u, h, :], ACT.Relu, bias=nt[:, u, h:h + 1], scale=-1.0,
                                         accum_out=den[:, u, h:h + 1])
                ins.then_inc(p_done.sem, 1)

            def copy_turned(m, u, r, t):
                n = 2 * m + u
                kn = KEYS[t][1]
                f = NK * r + t
                if f % 2 == 0:
                    act.wait_ge(*ov_done.at(n, r - 1))
                    act.wait_ge(*tr_done.at(n, f + 1))
                    act.activation(pT[0:kn, r % 2, t, :], tr[0][0:kn, 0:4 * S], ACT.Copy).then_inc(ca_done.sem, 1)

            def copy_out(m, u):
                n = 2 * m + u
                act.wait_ge(*ov_done.at(n, 4))
                act.wait_ge(*yo_done.at(n, -1))
                act.activation(oT[:, u, :], ov[:, 0:KD * S], ACT.Copy).then_inc(oT_done.sem, 1)

            def sequence(m, u, behind=True, here=True, ahead=True):
                following = (m, 1) if u == 0 else (m + 1, 0)
                if ahead:
                    copy_proj(*following, 0)
                for s in range(2 * newton if here else 5):
                    sums(m, u, s, here, following if ahead else None, prev(m, u) if behind else None)
                    if ahead and s < 2:
                        copy_proj(*following, 2 * s + 1)
                        copy_proj(*following, 2 * s + 2)
                    if behind and s == 4:
                        copy_out(*prev(m, u))
                if here:
                    probabilities(m, u, 0)
                    probabilities(m, u, 1)

            for f in range(5):
                copy_proj(0, 0, f)
            for h in range(H):
                copy_scores(0, 0, h)
            passes(act, sequence)

        @block.vector
        def _(dve):
            open_all(dve, v_done, cand_done, high_done, start_done, t_done, count_done, worst_done, cd_done, z_done,
                     st_done, mv_done)
            dve.memset(worst[:, :], 0.0).then_inc(cleared, 1)
            dve.wait_ge(cleared, 1)
            dve.wait_ge(w_in, 16 * LOADS)
            dve.wait_ge(setup, 4)

            def copy_v(m, u):
                n = 2 * m + u
                dve.wait_ge(*ov_done.at(n, -4))
                for t, (k0, kn) in enumerate(KEYS):
                    dve.wait_ge(*proj_done.at(n, 6 + t))
                    split = lambda ap: ap.rearrange("p (g e d) -> p g e d", e=2, d=HD)
                    for e in range(2):
                        ins = dve.tensor_tensor(vm[0:kn, u, t, e:H:2, HD * e:HD * e + HD],
                                                split(proj[(5 + t) % 2][0:kn, 0:D])[:, :, e, :],
                                                split(bvs[0:kn, :])[:, :, e, :], ALU.add)
                    ins.then_inc(v_done.sem, 1)

            def candidates(m, u, h):
                n = 2 * m + u
                stand(dve, turns, *sc_done.at(n, h + 1))
                for q, (k0, kn) in enumerate(PARTS):
                    ins = dve.max(cand[:, h, 8 * q:8 * q + 8], sc[h % SC][0:S, k0:k0 + kn])
                ins.then_inc(cand_done.sem, 1)
                dve.wait_ge(*cand_done.at(n, h + 1))
                dve.tensor_reduce(high[:, h:h + 1], cand[:, h, 0:NC:8], AX.X, ALU.max).then_inc(high_done.sem, 1)

            def start_step(m, u, e, chain, k):
                n = 2 * m + u
                hs = slice(HALF * e, HALF * e + HALF)
                t, c, o, ab = nt[:, u, hs], cand[:, hs, :], over[:, hs, :], above[:, hs, :]
                if k == 0:
                    stand(dve, turns, *high_done.at(n, HALF * e + HALF))
                    ins = dve.tensor_tensor(c, c, last_bcast(high[:, hs], NC), ALU.subtract)
                else:
                    chain.wait()
                if k == 1:
                    dve.tensor_scalar(ab, c, -1.0, None, ALU.is_gt)
                    ins = dve.tensor_scalar(o, c, 1.0, 0.0, ALU.add, ALU.max)
                if k == 6:
                    ins = dve.tensor_tensor(o, c, last_bcast(t, NC), ALU.add)
                if k == 7:
                    dve.tensor_scalar(ab, o, 0.0, None, ALU.is_gt)
                    ins = dve.tensor_scalar(o, o, 0.0, None, ALU.max)
                if k in (2, 8):
                    dve.tensor_reduce(ccount[:, hs], ab, AX.X, ALU.add)
                    ins = dve.tensor_reduce(csum[:, hs], o, AX.X, ALU.add)
                if k in (3, 9):
                    ins = dve.reciprocal(ccount[:, hs], ccount[:, hs])
                if k in (4, 10):
                    ins = dve.scalar_tensor_tensor(csum[:, hs], csum[:, hs], -1.0, ccount[:, hs], ALU.add, ALU.mult)
                if k == 5:
                    ins = dve.tensor_scalar(t, csum[:, hs], -1.0, 1.0, ALU.mult, ALU.add)
                if k < START - 1:
                    chain.count(ins)
                else:
                    dve.tensor_tensor(t, t, csum[:, hs], ALU.subtract).then_inc(start_done.sem, 1)
                    chain.end()

            def counts(m, u, s, chain, here, find, start, turned):
                n = 2 * m + u
                e = s % 2
                if here:
                    if s < 2:
                        dve.wait_ge(*z_in.at(n, HALF * e + HALF))
                        stand(dve, turns, *start_done.at(n, e + 1))
                    else:
                        stand(dve, turns, *t_done.at(n, s - 1))
                    stand(dve, turns, *count_done.at(n, s - 1))
                for j in range(HALF):
                    h = HALF * e + j
                    if here:
                        ins = dve.tensor_scalar(spare_d[:, e, j, :], zs[:, u, h, :], nt[:, u, h:h + 1], 0.0, ALU.is_lt,
                                                ALU.add, accum_out=count[:, h:h + 1])
                        if j == HALF - 1:
                            ins.then_inc(count_done.sem, 1)
                        if s and j >= STEP_AT:
                            step(m, u, s - 1, chain, j - STEP_AT)
                    if find and s in (4, 5) and HALF * (s - 4) + j < START:
                        start_step(*find, 0, start, HALF * (s - 4) + j)
                    if j % 2 and find and 2 <= s < 6:
                        candidates(*find, 4 * (s - 2) + j // 2)
                    if j in TURNED and turned and s < 4:
                        copy_turned(*turned, s, TURNED.index(j))

            def step(m, u, s, chain, k):
                n = 2 * m + u
                b, e = HALF * (s % 2), HALF * (s % 2) + HALF
                if k == 0:
                    dve.wait_ge(*count_done.at(n, s + 1))
                    chain.count(dve.reciprocal(rec[:, b:e], count[:, b:e]))
                if k == 1:
                    dve.wait_ge(*total_done.at(n, s + 1))
                    chain.wait()
                    chain.count(dve.scalar_tensor_tensor(gain[:, b:e], total[:, b:e], -1.0, rec[:, b:e], ALU.add, ALU.mult))
                if k == 2:
                    chain.wait()
                    dve.tensor_tensor(nt[:, u, b:e], nt[:, u, b:e], gain[:, b:e], ALU.subtract).then_inc(t_done.sem, 1)

            def largest_sum(m, u):
                n = 2 * m + u
                dve.wait_ge(*p_done.at(n, 2))
                stand(dve, turns, *worst_done.at(n, 0))
                dve.tensor_tensor(worst[:, :], worst[:, :], den[:, u, :], ALU.max).then_inc(worst_done.sem, 1)

            def copy_turned(m, u, r, t):
                n = 2 * m + u
                kn = KEYS[t][1]
                f = NK * r + t
                if f % 2:
                    dve.wait_ge(*ov_done.at(n, r - 1))
                    dve.wait_ge(*tr_done.at(n, f + 1))
                    dve.tensor_copy(pT[0:kn, r % 2, t, :], tr[1][0:kn, 0:4 * S]).then_inc(cd_done.sem, 1)

            def output(m, u):
                n = 2 * m + u
                dve.wait_ge(*yo_done.at(n, 1))
                dve.wait_ge(*xb_done.at(n, 1))
                dve.wait_ge(*xn_done.at(n, -1))
                dve.tensor_tensor(z[:, u, :], yo[0:S, 0:D], xb[:, u, :], ALU.add).then_inc(z_done.sem, 1)
                dve.wait_ge(*z_done.at(n, 1))
                dve.bn_stats(stats[:, u, :], z[:, u, :]).then_inc(st_done.sem, 1)
                stand(dve, turns, *st_done.at(n, 1))
                dve.bn_aggr(mv[:, u, :], stats[:, u, :]).then_inc(mv_done.sem, 1)

            def start_chain(m, u, e):
                return Chain(dve, turns, cand_step, 2 * (2 * m + u) + e, START - 1)

            def sequence(m, u, behind=True, here=True, ahead=True):
                following = (m, 1) if u == 0 else (m + 1, 0)
                chain = Chain(dve, turns, newton_step, 2 * m + u, NEWTON_STEPS)
                start = start_chain(*following, 0)
                for s in range(2 * newton if here else 6):
                    counts(m, u, s, chain, here, following if ahead else None, start, prev(m, u) if behind else None)
                    if behind and s == 0:
                        largest_sum(*prev(m, u))
                    if ahead and s == 4:
                        copy_v(*following)
                    if behind and s == 5:
                        output(*prev(m, u))
                if here:
                    for k in range(3):
                        step(m, u, 2 * newton - 1, chain, k)
                    chain.end()
                if ahead:
                    start = start_chain(*following, 1)
                    for k in range(START):
                        start_step(*following, 1, start, k)

            for h in range(3 * H // 4):
                candidates(0, 0, h)
            copy_v(0, 0)
            for h in range(3 * H // 4, H):
                candidates(0, 0, h)
            for e in range(2):
                start = start_chain(0, 0, e)
                for k in range(START):
                    start_step(0, 0, e, start, k)
            passes(dve, sequence)
            dve.wait_ge(*worst_done.at(B, 0))
            dve.tensor_reduce(top[:, :], worst[:, :], AX.X, ALU.max).then_inc(top_step, 1)


def mixture_of_experts(nc, x, gate, shared, experts, consts, rows_in, rows_out, out):
    F = 512
    KF = F // P
    CUT = TILES // 2
    UP = 2 * KD * F
    WIDE = UP + KF * D
    with ExitStack() as ctx:
        a = Place(nc, ctx, "me")
        gw = a.sb("gw", [P, KD, E])
        sw = a.sb("sw", [P, WIDE])
        cs = a.sb("cs", [P, consts.shape[1]])
        rank = cs[:, 0:E]
        before = cs[:, E:E + P]
        whole = cs[:, E + P:E + P + TILES]
        tile_no = cs[:, E + P + TILES:]
        ident = a.sb("ident", [P, P])
        ones = a.sb("ones", [P, P])
        zeros = a.sb("zeros", [P, 2048])
        half = a.sb("half", [P, 1])
        xs = a.sb("xs", [P, TILES, D])
        xl = a.sb("xl", [P, 2, D])
        xlT = a.sb("xlT", [P, 2, D])
        acc = a.sb("acc", [P, TILES, D])
        lg = a.sb("lg", [P, TILES, E])
        high = a.sb("high", [P, TILES])
        gain = a.sb("gain", [P, TILES])
        hot = a.sb("hot", [P, TILES, E])
        sel = a.sb("sel", [P, TILES])
        base = a.sb("base", [P, TILES + 1, E])
        fill = a.sb("fill", [P, E, TILES])
        need = a.sb("need", [P, E])
        ends = a.sb("ends", [P, 2, 2 * E])
        off = a.sb("off", [P, E])
        where = a.sb("where", [P, TILES, E])
        slot = a.sb("slot", [P, TILES])
        slot_i = a.sb("slot_i", [P, TILES], I32)
        past = a.sb("past", [1, SLOTS, E])
        owner = a.sb("owner", [1, SLOTS])
        owner_i = a.sb("owner_i", [1, SLOTS], I32)
        scaled = a.sb("scaled", [P, 2, D])
        index = a.sb("index", [P, 2], I32)
        we = a.sb("we", [P, 2, UP])
        wd = a.sb("wd", [P, 2, WIDE - UP])
        xe = a.sb("xe", [P, 2, D])
        xeT = a.sb("xeT", [P, 2, D])
        sg = a.sb("sg", [P, 2, F])
        h = a.sb("h", [P, 2, F])
        hT = a.sb("hT", [P, 2, F])
        ye = a.sb("ye", [P, 2, D])
        yg = a.sb("yg", [P, 2, D])
        z = a.sb("z", [P, 2, D])
        stats = a.sb("stats", [P, 2, 6])
        mv = a.sb("mv", [P, 2, 2])
        rstd = a.sb("rstd", [P, 2, 1])
        nbias = a.sb("nbias", [P, 2, 1])
        xn = a.sb("xn", [P, 2, D])
        g = [a.psum(f"g{n}") for n in range(2)]
        up = [a.psum(f"up{n}") for n in range(2)]
        trx = a.psum("trx")
        trh = a.psum("trh")
        yo = [a.psum(f"yo{n}") for n in range(2)]

        turns = a.sem("turns")
        w_in = a.sem("w_in")
        sw_in = a.sem("sw_in")
        xs_in = a.sem("xs_in")
        zeros_out = a.sem("zeros_out")
        setup = a.sem("setup")
        xl_in = [Event(a, f"xl_in{n}", 1, unit=16) for n in range(2)]
        xtr_done = Event(a, "xtr_done", 1, 2)
        xT_done = Event(a, "xT_done", 1)
        lgp_done = Event(a, "lgp_done", 1, 2)
        lg_done = Event(a, "lg_done", 1, 1)
        high_done = a.sem("high_done")
        hot_done = a.sem("hot_done")
        count_done = a.sem("count_done")
        gain_done = a.sem("gain_done")
        slot_done = a.sem("slot_done")
        owner_done = a.sem("owner_done")
        route = a.sem("route")
        scaled_done = Event(a, "scaled_done", 1)
        index_done = Event(a, "index_done", 1)
        sent = [Event(a, f"sent{n}", 1, unit=16, one=0) for n in range(2)]
        we_in = [Event(a, f"we_in{n}", 1, unit=16) for n in range(2)]
        wd_in = [Event(a, f"wd_in{n}", 1, unit=16) for n in range(2)]
        xe_in = [Event(a, f"xe_in{n}", 1, unit=16) for n in range(2)]
        etr_done = Event(a, "etr_done", 1, 2)
        eT_done = Event(a, "eT_done", 1)
        g_done = Event(a, "g_done", 1, 2)
        up_done = Event(a, "up_done", 1, 2)
        sg_done = Event(a, "sg_done", 1, 2)
        h_done = Event(a, "h_done", 1, 2)
        htr_done = Event(a, "htr_done", 1, 2)
        hT_done = Event(a, "hT_done", 1)
        y_done = Event(a, "y_done", 1, 2)
        ye_done = Event(a, "ye_done", 1, 2)
        stored_y = [Event(a, f"stored_y{n}", 1, unit=16) for n in range(2)]
        got = [Event(a, f"got{n}", 1, unit=16, one=0) for n in range(2)]
        back_done = Event(a, "back_done", 1)
        z_done = Event(a, "z_done", 1, 2)
        st_done = Event(a, "st_done", 1)
        mv_done = Event(a, "mv_done", 1)
        xn_done = Event(a, "xn_done", 1, 2)
        stored = [Event(a, f"stored{n}", 1, unit=16) for n in range(2)]
        pool_step = a.sem("pool_step")

        x_t = x.rearrange("(t p) d -> t p d", p=P)
        out_t = out.rearrange("(t p) d -> t p d", p=P)
        rows_in_t = rows_in.rearrange("(t p) d -> t p d", p=P)
        rows_out_t = rows_out.rearrange("(t p) d -> t p d", p=P)

        def tiles(eng, body):
            body(0, 0)
            body(0, 1)
            with eng.Fori(1, TILES // 2) as m:
                body(m, 0)
                body(m, 1)
            body(TILES // 2, 0)

        def gate_w(w, k):
            return w[:, k * F:(k + 1) * F]

        def up_w(w, k):
            return w[:, (KD + k) * F:(KD + k + 1) * F]

        block = ctx.enter_context(nc.Block())

        @block.sync
        def _(sp):
            open_all(sp, *we_in, *wd_in, *xe_in, *stored, *xl_in)
            sp.dma_start(gw[:, :, :], gate.rearrange("(k p) n -> p k n", p=P)).then_inc(w_in, 16)
            sp.dma_start(cs[:, :], consts).then_inc(w_in, 16)
            sp.dma_start(xs[:, :, :], x.rearrange("(t p) d -> p t d", p=P)).then_inc(xs_in, 16)
            sp.dma_start(sw[:, :], shared).then_inc(sw_in, 16)

            for into, arrived, turned in ((xl, xl_in, xtr_done), (xe, xe_in, etr_done)):
                def load(m, u):
                    n = 2 * m + u
                    stand(sp, turns, *turned.at(n, -1))
                    sp.dma_start(into[:, u, :], x_t[n]).then_inc(arrived[u].sem, 16)

                tiles(sp, load)

            sp.wait_ge(owner_done, 1)
            with sp.Fori(0, SLOTS // 2) as m:
                for u in range(2):
                    j = 2 * m + u
                    e = sp.value_load(owner_i[0:1, bass.ds(j, 1)], min_val=0, max_val=E - 1)
                    stand(sp, turns, *up_done.at(TILES + j, -1))
                    sp.dma_start(we[:, u, :], experts[e][:, 0:UP]).then_inc(we_in[u].sem, 16)
                    if u == 0:
                        sp.wait_ge(*sent[0].at((TILES + 1) // 2, 0))
                        sp.wait_ge(*sent[1].at(TILES // 2, 0))
                    stand(sp, turns, *etr_done.at(TILES + j, -1))
                    sp.dma_start(xe[:, 1 - u, :], rows_in_t[j]).then_inc(xe_in[1 - u].sem, 16)
                    stand(sp, turns, *y_done.at(TILES + j, -1))
                    sp.dma_start(wd[:, u, :], experts[e][:, UP:]).then_inc(wd_in[u].sem, 16)

            with sp.Fori(0, TILES // 2) as m:
                for u in range(2):
                    n = 2 * m + u
                    stand(sp, turns, *xn_done.at(n, 1))
                    sp.dma_start(out_t[n], xn[:, u, :]).then_inc(stored[u].sem, 16)
            sp.wait_ge(*xn_done.at(TILES - 1, 1))
            sp.dma_start(out_t[TILES - 1], xn[:, 0, :]).then_inc(stored[0].sem, 16)
            sp.wait_ge(*stored[0].at((TILES + 1) // 2, 0))
            sp.wait_ge(*stored[1].at(TILES // 2, 0))

        @block.gpsimd
        def _(pool):
            open_all(pool, index_done, back_done, xn_done)
            identity(pool, ident, setup, 0)
            pool.memset(half[:, :], -0.5).then_inc(setup, 1)
            pool.memset(ones[:, :], 1.0).then_inc(setup, 1)
            pool.wait_ge(setup, 4)

            def send(m, u):
                n = 2 * m + u
                if not is_first(m):
                    stand(pool, turns, *sent[u].at(m, 0))
                pool.tensor_copy(index[:, u:u + 1], slot_i[:, bass.ds(n, 1)]).then_inc(index_done.sem, 1)
                pool.wait_ge(*scaled_done.at(n, 1))
                stand(pool, turns, *index_done.at(n, 1))
                pool.indirect_dma_start(rows_in, bass.IndirectOffsetOnAxis(ap=index[:, u:u + 1], axis=0),
                                        scaled[:, u, :], None).then_inc(sent[u].sem, 16)

            def fetch(m, u):
                n = 2 * m + u
                pool.wait_ge(*z_done.at(n, -1))
                if not is_first(m):
                    stand(pool, turns, *got[u].at(m, 0))
                pool.tensor_copy(index[:, u:u + 1], slot_i[:, bass.ds(n, 1)]).then_inc(back_done.sem, 1)
                stand(pool, turns, *back_done.at(n, 1))
                pool.indirect_dma_start(yg[:, u, :], None, rows_out,
                                        bass.IndirectOffsetOnAxis(ap=index[:, u:u + 1], axis=0)).then_inc(got[u].sem, 16)

            def norm(m, u):
                n = 2 * m + u
                chain = Chain(pool, turns, pool_step, n, NORM_STEPS)
                pool.wait_ge(*stored[u].at(m, 0))
                stand(pool, turns, *mv_done.at(n, 1))
                norm_rows(pool, chain, z[:, u, :], mv[:, u, :], rstd[:, u, :], nbias[:, u, :], half[:, :],
                          xn[:, u, :], xn_done.sem)
                chain.end()

            pool.wait_ge(slot_done, 1)
            pool.wait_ge(zeros_out, 16)
            tiles(pool, send)
            for u in range(2):
                pool.wait_ge(*sent[u].at((TILES + 1 - u) // 2, 0))
            for u in range(2):
                pool.wait_ge(*stored_y[u].at(SLOTS // 2, 0))
            fetch(0, 0)
            fetch(0, 1)
            norm(0, 0)
            fetch(1, 0)
            norm(0, 1)
            with pool.Fori(1, TILES // 2) as m:
                fetch(m, 1)
                norm(m, 0)
                fetch(m + 1, 0)
                norm(m, 1)
            norm(TILES // 2, 0)

        @block.tensor
        def _(pe):
            open_all(pe, xtr_done, lgp_done, etr_done, g_done, up_done, htr_done, y_done)
            pe.wait_ge(setup, 4)
            pe.wait_ge(w_in, 32)

            def turn_x(m, u):
                n = 2 * m + u
                pe.wait_ge(*xl_in[u].at(m, 1))
                pe.wait_ge(*xT_done.at(n, 0))
                for k in range(KD):
                    mm = pe.transpose(trx[:, k * P:(k + 1) * P], xl[:, u, k * P:(k + 1) * P], ident[:, :])
                mm.then_inc(xtr_done.sem, 1)

            def logits(m, u):
                n = 2 * m + u
                pe.wait_ge(*xT_done.at(n, 1))
                pe.wait_ge(*lg_done.at(n, 0))
                for k in range(KD):
                    mm = pe.matmul(g[u][:, 0:E], xlT[:, u, k * P:(k + 1) * P], gw[:, k, :],
                                   start=(k == 0), stop=(k == KD - 1))
                mm.then_inc(lgp_done.sem, 1)

            def turn_logits(m, u):
                turn_x(m, u)
                logits(m, u)

            tiles(pe, turn_logits)

            pe.wait_ge(hot_done, 1)
            for c, (t0, t1) in enumerate(((0, CUT), (CUT, TILES))):
                pe.matmul(up[c][:, 0:(t1 - t0) * E], before, hot[:, t0:t1, :], start=True, stop=True)
                pe.matmul(g[c][:, 0:(t1 - t0) * E], ones[:, :], hot[:, t0:t1, :],
                          start=True, stop=True).then_inc(count_done, 1)

            def turn_rows(n, i, u):
                pe.wait_ge(*xe_in[u].at(i, 1))
                pe.wait_ge(*eT_done.at(n, 0))
                for k in range(KD):
                    mm = pe.transpose(trx[:, k * P:(k + 1) * P], xe[:, u, k * P:(k + 1) * P], ident[:, :])
                mm.then_inc(etr_done.sem, 1)

            def gate_up(n, u, w):
                pe.wait_ge(*eT_done.at(n, 1))
                pe.wait_ge(*sg_done.at(n, -1))
                stand(pe, turns, *h_done.at(n, -1))
                for k in range(KD):
                    mm = pe.matmul(g[u][:, :], xeT[:, u, k * P:(k + 1) * P], gate_w(w, k), start=(k == 0), stop=(k == KD - 1))
                mm.then_inc(g_done.sem, 1)
                for k in range(KD):
                    mm = pe.matmul(up[u][:, :], xeT[:, u, k * P:(k + 1) * P], up_w(w, k), start=(k == 0), stop=(k == KD - 1))
                mm.then_inc(up_done.sem, 1)

            def down(n, u, w):
                pe.wait_ge(*h_done.at(n, 1))
                pe.wait_ge(*hT_done.at(n, 0))
                for k in range(KF):
                    mm = pe.transpose(trh[:, k * P:(k + 1) * P], h[:, u, k * P:(k + 1) * P], ident[:, :])
                mm.then_inc(htr_done.sem, 1)
                pe.wait_ge(*hT_done.at(n, 1))
                pe.wait_ge(*ye_done.at(n, -1))
                for k in range(KF):
                    mm = pe.matmul(yo[u][:, 0:D], hT[:, u, k * P:(k + 1) * P], w[:, k * D:(k + 1) * D], start=(k == 0), stop=(k == KF - 1))
                mm.then_inc(y_done.sem, 1)

            def shared_up(m, u):
                n = 2 * m + u
                turn_rows(n, m, u)
                gate_up(n, u, sw)

            def shared_down(m, u):
                down(2 * m + u, u, sw[:, UP:])

            pe.wait_ge(sw_in, 16)
            pe.wait_ge(slot_done, 1)
            shared_up(0, 0)
            with pe.Fori(0, TILES // 2) as m:
                shared_up(m, 1)
                shared_down(m, 0)
                shared_up(m + 1, 0)
                shared_down(m, 1)
            shared_down(TILES // 2, 0)

            def expert_up(m, u):
                n = TILES + 2 * m + u
                turn_rows(n, TILES // 2 + u + m, 1 - u)
                pe.wait_ge(*we_in[u].at(m, 1))
                gate_up(n, 1 - u, we[:, u, :])

            def expert_down(m, u):
                pe.wait_ge(*wd_in[u].at(m, 1))
                down(TILES + 2 * m + u, 1 - u, wd[:, u, :])

            expert_up(0, 0)
            with pe.Fori(0, SLOTS // 2 - 1) as m:
                expert_up(m, 1)
                expert_down(m, 0)
                expert_up(m + 1, 0)
                expert_down(m, 1)
            expert_up(SLOTS // 2 - 1, 1)
            expert_down(SLOTS // 2 - 1, 0)
            expert_down(SLOTS // 2 - 1, 1)

        @block.scalar
        def _(act):
            open_all(act, xT_done, scaled_done, sg_done, hT_done, eT_done, *stored_y)
            act.wait_ge(setup, 5)
            act.dma_start(rows_in.rearrange("(p a b) d -> p a (b d)", p=P, b=2048 // D),
                          mid_bcast(zeros[:, :], SLOTS * D // 2048)).then_inc(zeros_out, 16)

            def copy_x(m, u):
                n = 2 * m + u
                act.wait_ge(*xtr_done.at(n, 1))
                act.wait_ge(*lgp_done.at(n, -1))
                act.activation(xlT[:, u, :], trx[:, 0:D], ACT.Copy).then_inc(xT_done.sem, 1)

            tiles(act, copy_x)
            act.wait_ge(xs_in, 16)
            act.wait_ge(high_done, 1)
            act.activation(gain[:, :], high[:, :], ACT.Sigmoid).then_inc(gain_done, 1)
            act.wait_ge(gain_done, 1)

            def scale_rows(m, u):
                n = 2 * m + u
                if not is_first(m):
                    stand(act, turns, *sent[u].at(m, 0))
                act.activation(scaled[:, u, :], xs[:, bass.ds(n, 1), :].rearrange("p t d -> p (t d)"), ACT.Copy,
                               scale=gain[:, bass.ds(n, 1)]).then_inc(scaled_done.sem, 1)

            def silu(n, u):
                act.wait_ge(*g_done.at(n, 1))
                act.wait_ge(*h_done.at(n, -1))
                act.activation(sg[:, u, :], g[u][:, :], ACT.Silu).then_inc(sg_done.sem, 1)

            def copy_h(n, u):
                act.wait_ge(*htr_done.at(n, 1))
                act.wait_ge(*y_done.at(n, -1))
                act.activation(hT[:, u, :], trh[:, :], ACT.Copy).then_inc(hT_done.sem, 1)

            def copy_e(n, u):
                act.wait_ge(*etr_done.at(n, 1))
                act.wait_ge(*up_done.at(n, -1))
                act.activation(xeT[:, u, :], trx[:, 0:D], ACT.Copy).then_inc(eT_done.sem, 1)

            def shared_pair(m):
                scale_rows(m, 1)
                copy_e(2 * m + 1, 1)
                silu(2 * m + 1, 1)
                copy_h(2 * m, 0)
                scale_rows(m + 1, 0)
                copy_e(2 * m + 2, 0)
                silu(2 * m + 2, 0)
                copy_h(2 * m + 1, 1)

            scale_rows(0, 0)
            copy_e(0, 0)
            silu(0, 0)
            shared_pair(0)
            with act.Fori(1, TILES // 2) as m:
                shared_pair(m)
            copy_h(TILES - 1, 0)

            def store_y(m, u):
                stand(act, turns, *ye_done.at(TILES + 2 * m + u, 1))
                act.dma_start(rows_out_t[2 * m + u], ye[:, u, :]).then_inc(stored_y[u].sem, 16)

            copy_e(TILES, 1)
            silu(TILES, 1)
            with act.Fori(0, SLOTS // 2 - 1) as m:
                copy_e(TILES + 2 * m + 1, 0)
                silu(TILES + 2 * m + 1, 0)
                copy_h(TILES + 2 * m, 1)
                copy_e(TILES + 2 * m + 2, 1)
                store_y(m, 0)
                silu(TILES + 2 * m + 2, 1)
                copy_h(TILES + 2 * m + 1, 0)
                store_y(m, 1)
            LAST = SLOTS // 2 - 1
            copy_e(TILES + 2 * LAST + 1, 0)
            silu(TILES + 2 * LAST + 1, 0)
            copy_h(TILES + 2 * LAST, 1)
            store_y(LAST, 0)
            copy_h(TILES + 2 * LAST + 1, 0)
            store_y(LAST, 1)

        @block.vector
        def _(dve):
            open_all(dve, lg_done, h_done, ye_done, z_done, st_done, mv_done)
            dve.wait_ge(setup, 4)
            dve.memset(zeros[:, :], 0.0).then_inc(setup, 1)
            dve.wait_ge(w_in, 32)

            def copy_logits(m, u):
                n = 2 * m + u
                stand(dve, turns, *lgp_done.at(n, 1))
                dve.tensor_copy(lg[:, bass.ds(n, 1), :], g[u][:, 0:E].unsqueeze(1)).then_inc(lg_done.sem, 1)

            tiles(dve, copy_logits)
            dve.wait_ge(*lg_done.at(TILES, 0))

            steps = [0]

            def then(ins):
                ins.then_inc(route, 1)
                steps[0] += 1
                dve.wait_ge(route, steps[0])

            dve.tensor_reduce(high[:, :], lg[:, :, :], AX.X, ALU.max).then_inc(high_done, 1)
            dve.wait_ge(high_done, 1)
            then(dve.tensor_tensor(hot[:, :, :], lg[:, :, :], last_bcast(high[:, :], E), ALU.is_equal))
            then(dve.tensor_tensor(hot[:, :, :], hot[:, :, :], mid_bcast(rank, TILES), ALU.mult))
            then(dve.tensor_reduce(sel[:, :], hot[:, :, :], AX.X, ALU.max))
            dve.tensor_tensor(hot[:, :, :], mid_bcast(rank, TILES), last_bcast(sel[:, :], E), ALU.is_equal).then_inc(hot_done, 1)
            then(dve.memset(base[:, 0, :], 0.0))
            dve.wait_ge(count_done, 2)
            rows = lambda banks, t: banks[t >= CUT][:, (t - CUT * (t >= CUT)) * E:(t + 1 - CUT * (t >= CUT)) * E]
            for t in range(TILES):
                then(dve.tensor_tensor(base[:, t + 1, :], base[:, t, :], rows(g, t), ALU.add))
            then(dve.tensor_tensor(fill[:, :, :], last_bcast(base[:, TILES, :], TILES), mid_bcast(whole, E), ALU.is_gt))
            then(dve.memset(ends[:, :, :], 0.0))
            then(dve.tensor_reduce(need[:, :], fill[:, :, :], AX.X, ALU.add))
            then(dve.tensor_copy(ends[:, 0, E:2 * E], need[:, :]))
            side = 0
            d = 1
            while d < E:
                then(dve.tensor_tensor(ends[:, 1 - side, E:2 * E], ends[:, side, E:2 * E], ends[:, side, E - d:2 * E - d], ALU.add))
                side, d = 1 - side, 2 * d
            end = ends[:, side, E:2 * E]
            then(dve.tensor_tensor(past[:, :, :], mid_bcast(ends[0:1, side, E:2 * E], SLOTS), last_bcast(tile_no[0:1, :], E), ALU.is_le))
            then(dve.tensor_reduce(owner[:, :], past[:, :, :], AX.X, ALU.add))
            then(dve.tensor_scalar(owner[:, :], owner[:, :], E - 1.0, None, ALU.min))
            dve.tensor_copy(owner_i[:, :], owner[:, :]).then_inc(owner_done, 1)
            then(dve.tensor_tensor(off[:, :], end, need[:, :], ALU.subtract))
            then(dve.tensor_scalar(off[:, :], off[:, :], float(P), None, ALU.mult))
            then(dve.tensor_tensor(where[:, :, :], base[:, 0:TILES, :], mid_bcast(off[:, :], TILES), ALU.add))
            for c, (t0, t1) in enumerate(((0, CUT), (CUT, TILES))):
                then(dve.tensor_tensor(where[:, t0:t1, :], where[:, t0:t1, :],
                                       up[c][:, 0:(t1 - t0) * E].rearrange("p (t e) -> p t e", e=E), ALU.add))
            then(dve.tensor_tensor(where[:, :, :], where[:, :, :], hot[:, :, :], ALU.mult))
            then(dve.tensor_reduce(slot[:, :], where[:, :, :], AX.X, ALU.add))
            dve.tensor_copy(slot_i[:, :], slot[:, :]).then_inc(slot_done, 1)

            def times_up(n, u):
                dve.wait_ge(*up_done.at(n, 1))
                dve.wait_ge(*sg_done.at(n, 1))
                dve.wait_ge(*htr_done.at(n, -1))
                dve.tensor_tensor(h[:, u, :], sg[:, u, :], up[u][:, :], ALU.mult).then_inc(h_done.sem, 1)

            def add_shared(m, u):
                n = 2 * m + u
                stand(dve, turns, *y_done.at(n, 1))
                dve.tensor_tensor(acc[:, bass.ds(n, 1), :], xs[:, bass.ds(n, 1), :], yo[u][:, 0:D].unsqueeze(1),
                                  ALU.add).then_inc(ye_done.sem, 1)

            dve.wait_ge(xs_in, 16)
            times_up(0, 0)
            with dve.Fori(0, TILES // 2) as m:
                times_up(2 * m + 1, 1)
                add_shared(m, 0)
                times_up(2 * m + 2, 0)
                add_shared(m, 1)
            add_shared(TILES // 2, 0)

            def copy_y(m, u):
                n = TILES + 2 * m + u
                dve.wait_ge(*y_done.at(n, 1))
                dve.wait_ge(*stored_y[u].at(m, 0))
                dve.tensor_copy(ye[:, u, :], yo[1 - u][:, 0:D]).then_inc(ye_done.sem, 1)

            times_up(TILES, 1)
            with dve.Fori(0, SLOTS // 2 - 1) as m:
                times_up(TILES + 2 * m + 1, 0)
                copy_y(m, 0)
                times_up(TILES + 2 * m + 2, 1)
                copy_y(m, 1)
            LAST = SLOTS // 2 - 1
            times_up(TILES + 2 * LAST + 1, 0)
            copy_y(LAST, 0)
            copy_y(LAST, 1)

            def output(m, u):
                n = 2 * m + u
                dve.wait_ge(*got[u].at(m, 1))
                stand(dve, turns, *xn_done.at(n, -1))
                dve.tensor_tensor(z[:, u:u + 1, :], acc[:, bass.ds(n, 1), :], yg[:, u:u + 1, :], ALU.add).then_inc(z_done.sem, 1)
                dve.wait_ge(*z_done.at(n, 1))
                dve.bn_stats(stats[:, u, :], z[:, u, :]).then_inc(st_done.sem, 1)
                stand(dve, turns, *st_done.at(n, 1))
                dve.bn_aggr(mv[:, u, :], stats[:, u, :]).then_inc(mv_done.sem, 1)

            dve.wait_ge(*ye_done.at(TILES, 0))
            tiles(dve, output)


SUM_ERROR = 2.0 ** -17


def unfinished(nc, sum_max, flag):
    with ExitStack() as ctx:
        a = Place(nc, ctx, "uf")
        row = a.sb("row", [1, S])
        high = a.sb("high", [1, 1])
        late = a.sb("late", [1, 1])
        row_in = a.sem("row_in")
        step = a.sem("step")
        block = ctx.enter_context(nc.Block())

        @block.sync
        def _(sp):
            sp.dma_start(row[:, :], sum_max.rearrange("s o -> o s")).then_inc(row_in, 16)

        @block.vector
        def _(dve):
            dve.wait_ge(row_in, 16)
            dve.tensor_reduce(high[:, :], row[:, :], AX.X, ALU.max).then_inc(step, 1)
            dve.wait_ge(step, 1)
            dve.tensor_scalar(late[:, :], high[:, :], 1.0 + SUM_ERROR, None, ALU.is_gt).then_inc(step, 1)
            dve.wait_ge(step, 2)
            dve.tensor_copy(flag, late[:, :]).then_inc(step, 1)
            dve.wait_ge(step, 3)


def build(nc, t):
    dram = lambda name, shape: nc.dram_tensor(name, shape, F32, kind="Internal").ap()
    rows = [dram(f"rows{n}", (ROWS, D)) for n in range(5)]
    tanh_attention(nc, t["x"], t["xT"], t["a0_Wq"], t["a0_bq"], t["a0_Wk"], t["a0_bk"], t["a0_Wv"], t["a0_bv"],
                   t["a0_Wo"], t["a0_bo"], rows[0])
    cross_attention(nc, rows[0], t["cT"], t["mask"], t["heads01"], t["c0_WqT"], t["c0_WkT"], t["c0_WvT"],
                    t["c0_WoT"], t["c0_bo"], rows[1])
    quantised_linear(nc, rows[1], t["f0_W"], t["f0_bias"], rows[2])
    normed_attention(nc, rows[2], t["heads01"], t["causal"], t["a1_WkqT"], t["a1_WvT"], t["a1_WuT"],
                     t["a1_ln_w"], t["a1_ln_b"], rows[3])
    sums = [dram(f"sum_max{n}", (S, 1)) for n in range(2)]
    sparse = lambda newton, tag, sum_max: sparse_attention(
        nc, rows[3], t["cT"], t["heads4"], t["c1_Wq"], t["c1_bq"], t["c1_Wk"], t["c1_bk"], t["c1_Wv"], t["c1_bv"],
        t["c1_Wo"], t["c1_bo"], rows[4], sum_max, newton, tag)
    sparse(FEW_STEPS, "sa", sums[0])
    with nc.sbuf_tensor("late", [1, 1], I32) as flag:
        unfinished(nc, sums[0], flag[:, :])
        late = nc.values_load(flag[0:1, 0:1], min_val=0, max_val=1)
        with nc.If(late == 1):
            sparse(ALL_STEPS, "sb", sums[1])
        mixture_of_experts(nc, rows[4], t["m_gate"], t["m_shared"], t["m_experts"], t["m_consts"],
                           dram("rows_in", (SLOTS * P, D)), dram("rows_out", (SLOTS * P, D)), t["out"])


def kernel(**inputs):
    from concourse import bacc
    from concourse.bass_utils import run_bass_kernel_spmd

    whole = np.ascontiguousarray
    every = lambda v: np.tile(v, (P, 1))
    split = lambda v: whole(v.reshape(-1, P).T)
    x = inputs["x"].reshape(ROWS, D)
    ctx_rows = inputs["ctx_1024"]
    a0, c0, f0, a1, c1, m = (
        {name[len(block):]: v for name, v in inputs.items() if name.startswith(block)}
        for block in ("L0_attn_", "L0_xattn_", "L0_ffn_", "L1_attn_", "L1_xattn_", "L1_ffn_"))
    heads01 = np.equal(np.arange(P)[:, None] // 16, np.arange(P // 16)).astype(np.float32)
    heads4 = np.where(heads01 > 0, np.float32(0.25), np.float32(0))
    causal = np.where(np.tri(S, dtype=bool), np.float32(0), np.float32(-1e30))

    def chunks(w):
        e, k, n = w.shape
        return w.reshape(e, k // P, P, n).transpose(0, 2, 1, 3).reshape(e, P, -1)

    def swiglu(gate, up, down):
        return whole(np.concatenate([chunks(gate), chunks(up), chunks(down)], axis=2))

    m_consts = np.concatenate([every(E - np.arange(E)), np.triu(np.ones((P, P)), 1), every(P * np.arange(TILES)),
                               every(np.arange(SLOTS))], axis=1).astype(np.float32)
    arrays = {
        "x": whole(x), "xT": whole(x.T), "cT": whole(ctx_rows.transpose(0, 2, 1)),
        "mask": whole(inputs["mask_Bx1xSxS2_ik1"][:, 0]),
        "heads01": heads01, "heads4": heads4, "causal": causal,
        "a0_Wq": a0["Wq"], "a0_bq": split(a0["bq"]), "a0_Wk": a0["Wk"], "a0_bk": split(a0["bk"]),
        "a0_Wv": a0["Wv"], "a0_bv": every(a0["bv"]), "a0_Wo": a0["Wo"], "a0_bo": every(a0["bo"]),
        "c0_WqT": whole(c0["Wq"].T), "c0_WkT": whole(c0["Wk"].T), "c0_WvT": whole(c0["Wv"].T),
        "c0_WoT": whole(c0["Wo"].T), "c0_bo": every(c0["bo"]),
        "f0_W": f0["weight"], "f0_bias": every(f0["bias"]),
        "a1_WkqT": np.concatenate([a1["Wk"].T, a1["Wq"].T], axis=1), "a1_WvT": whole(a1["Wv"].T),
        "a1_WuT": whole(a1["Wu"].T),
        "a1_ln_w": every(np.concatenate([np.tile(a1["kln_w"], 16), np.tile(a1["qln_w"], 16)])),
        "a1_ln_b": every(np.concatenate([np.tile(a1["kln_b"], 16), np.tile(a1["qln_b"], 16)])),
        "c1_Wq": c1["Wq"], "c1_bq": split(c1["bq"]), "c1_Wk": c1["Wk"], "c1_bk": split(c1["bk"]),
        "c1_Wv": c1["Wv"], "c1_bv": every(c1["bv"]), "c1_Wo": c1["Wo"], "c1_bo": every(c1["bo"]),
        "m_gate": m["gate_w"],
        "m_shared": swiglu(m["shared_gate_w"][None], m["shared_up_w"][None], m["shared_down_w"][None])[0],
        "m_experts": swiglu(m["routed_gate_w"], m["routed_up_w"], m["routed_down_w"]),
        "m_consts": m_consts,
    }
    nc = bacc.Bacc("TRN2", target_bir_lowering=False, num_devices=1)
    t = {name: nc.dram_tensor(name, a.shape, mybir.dt.from_np(a.dtype), kind="ExternalInput").ap()
         for name, a in arrays.items()}
    t["out"] = nc.dram_tensor("out", (ROWS, D), F32, kind="ExternalOutput").ap()
    build(nc, t)
    return run_bass_kernel_spmd(nc, [arrays], core_ids=[0]).results[0]["out"].reshape(B, S, D)
```
